# Optimizing a Trainium2 kernel written in Bass

```python
import numpy as np
import jax
import jax.numpy as jnp

def _softmax(x, axis=-1):
    return jax.nn.softmax(x, axis=axis)

def _gelu(x):
    return jax.nn.gelu(x, approximate=True)

def _silu(x):
    return jax.nn.silu(x)

def _sigmoid(x):
    return jax.nn.sigmoid(x)

def _layernorm(x, axis=-1, eps=1e-05):
    m = jnp.mean(x, axis=axis, keepdims=True)
    v = jnp.var(x, axis=axis, keepdims=True)
    return (x - m) / jnp.sqrt(v + eps)

def _scatter_add(tgt, idx, src, axis=0):
    return tgt.at[idx].add(src)

def _segment_sum(src, seg, n):
    return jax.ops.segment_sum(src, seg, n)
kernel_name = 'mk_prb_d1_jaxref_r8_d8fdde'

def setup_inputs(seed: int=0):
    np.random.seed(seed)
    _w = jnp.asarray

    def _L0_attn_setup():
        import jax, jax.numpy as jnp
        import numpy as np
        FEATS = 128
        HEAD = 16
        HEAD_DIM = FEATS // HEAD
        EPS = 1e-12

        def _l2norm(t):
            n = jnp.sqrt(jnp.sum(t * t, axis=-1, keepdims=True))
            return t / jnp.maximum(n, EPS)
        key = jax.random.key(seed)
        ks = jax.random.split(key, 10)
        s = 0.02
        inp = {'x': jax.random.normal(ks[0], (4, 256, FEATS), dtype=jnp.float32), 'Wq': jax.random.normal(ks[1], (FEATS, FEATS), dtype=jnp.float32) * s, 'bq': jnp.zeros((FEATS,), dtype=jnp.float32), 'Wk': jax.random.normal(ks[2], (FEATS, FEATS), dtype=jnp.float32) * s, 'bk': jnp.zeros((FEATS,), dtype=jnp.float32), 'Wv': jax.random.normal(ks[3], (FEATS, FEATS), dtype=jnp.float32) * s, 'bv': jnp.zeros((FEATS,), dtype=jnp.float32), 'Wo': jax.random.normal(ks[4], (FEATS, FEATS), dtype=jnp.float32) * s, 'bo': jnp.zeros((FEATS,), dtype=jnp.float32), 'm': jnp.full((HEAD,), 0.5, dtype=jnp.float32)}
        return inp
    _L0_attn_in = _L0_attn_setup()

    def _L0_ffn_setup():
        import jax, jax.numpy as jnp
        import numpy as np
        D_MODEL = 128
        HIDDEN = 512
        N_EXPERTS = 8
        TOP_K = 2
        key = jax.random.key(seed)
        k_x, k_r, k_w1, k_w2 = jax.random.split(key, 4)
        x = jax.random.normal(k_x, (2, 128, D_MODEL), dtype=jnp.float32)
        Wr = jax.random.normal(k_r, (D_MODEL, N_EXPERTS), dtype=jnp.float32) * 0.02
        W1 = jax.random.normal(k_w1, (N_EXPERTS, D_MODEL, HIDDEN), dtype=jnp.float32) * 0.02
        W2 = jax.random.normal(k_w2, (N_EXPERTS, HIDDEN, D_MODEL), dtype=jnp.float32) * 0.02
        return {'x': x, 'Wr': Wr, 'W1': W1, 'W2': W2}
    _L0_ffn_in = _L0_ffn_setup()
    _d = {'L0_attn_x': _L0_attn_in['x'], 'L0_attn_Wq': _L0_attn_in['Wq'], 'L0_attn_bq': _L0_attn_in['bq'], 'L0_attn_Wk': _L0_attn_in['Wk'], 'L0_attn_bk': _L0_attn_in['bk'], 'L0_attn_Wv': _L0_attn_in['Wv'], 'L0_attn_bv': _L0_attn_in['bv'], 'L0_attn_Wo': _L0_attn_in['Wo'], 'L0_attn_bo': _L0_attn_in['bo'], 'L0_attn_m': _L0_attn_in['m'], 'L0_ffn_Wr': _L0_ffn_in['Wr'], 'L0_ffn_W1': _L0_ffn_in['W1'], 'L0_ffn_W2': _L0_ffn_in['W2']}
    _x0 = _d['L0_attn_x']
    _d['L0_attn_x'] = jax.random.normal(jax.random.fold_in(jax.random.key(seed), 1), (32, 256, 128), dtype=_x0.dtype)
    del _x0
    return _d

def reference(L0_attn_x, L0_attn_Wq, L0_attn_bq, L0_attn_Wk, L0_attn_bk, L0_attn_Wv, L0_attn_bv, L0_attn_Wo, L0_attn_bo, L0_attn_m, L0_ffn_Wr, L0_ffn_W1, L0_ffn_W2):

    def _L0_attn_ref(x, Wq, bq, Wk, bk, Wv, bv, Wo, bo, m):
        import jax, jax.numpy as jnp
        import numpy as np
        FEATS = 128
        HEAD = 16
        HEAD_DIM = FEATS // HEAD
        EPS = 1e-12

        def _l2norm(t):
            n = jnp.sqrt(jnp.sum(t * t, axis=-1, keepdims=True))
            return t / jnp.maximum(n, EPS)
        b, n, f = x.shape

        def proj(W, bias):
            y = x @ W + bias
            return y.reshape(b, n, HEAD, HEAD_DIM).transpose(0, 2, 1, 3)
        q = _l2norm(proj(Wq, bq))
        k = _l2norm(proj(Wk, bk))
        v = proj(Wv, bv)
        sim = jnp.einsum('bhid,bhjd->bhij', q, k)
        sigma_m = jax.nn.sigmoid(m).reshape(1, HEAD, 1, 1)
        scaling = jnp.asarray(n, dtype=x.dtype) ** sigma_m
        attn = sim / scaling
        out = jnp.einsum('bhij,bhjd->bhid', attn, v)
        out = out.transpose(0, 2, 1, 3).reshape(b, n, f)
        return out @ Wo + bo

    def _L0_ffn_ref(x, Wr, W1, W2):
        import jax, jax.numpy as jnp
        import numpy as np
        D_MODEL = 128
        HIDDEN = 512
        N_EXPERTS = 8
        TOP_K = 2
        B, S, D = x.shape
        flat = x.reshape(-1, D)
        logits = flat @ Wr
        top_vals, top_idx = jax.lax.top_k(logits, TOP_K)
        weights = jax.nn.softmax(top_vals, axis=-1)
        top1 = top_idx[:, 0]
        w_top1 = weights[:, 0]
        h = jax.nn.gelu(jnp.einsum('td,edh->teh', flat, W1), approximate=False)
        y = jnp.einsum('teh,ehd->ted', h, W2)
        y_sel = jnp.take_along_axis(y, top1[:, None, None], axis=1)[:, 0, :]
        out = (w_top1[:, None] * y_sel).reshape(B, S, D)
        return out
    x = L0_attn_x
    xn = _layernorm(x, axis=-1)
    x = x + _L0_attn_ref(xn, L0_attn_Wq, L0_attn_bq, L0_attn_Wk, L0_attn_bk, L0_attn_Wv, L0_attn_bv, L0_attn_Wo, L0_attn_bo, L0_attn_m) + _L0_ffn_ref(xn, L0_ffn_Wr, L0_ffn_W1, L0_ffn_W2)
    return x

_drawn_inputs = setup_inputs


def setup_inputs(seed=0):
    import zlib

    import numpy as np

    out = dict(_drawn_inputs(seed))
    spreads = {'L0_attn_bq': (0.0, 0.642),
     'L0_attn_bk': (0.0, 0.312),
     'L0_attn_bv': (0.0, 0.311),
     'L0_attn_bo': (0.0, 0.1),
     'L0_attn_m': (0.5, 0.6)}
    factors = {'L0_attn_Wk': 3.613, 'L0_attn_Wv': 3.775}
    for name, (base, spread) in spreads.items():
        noise = np.random.default_rng([zlib.crc32(name.encode()), seed]).standard_normal(out[name].shape)
        drawn = base * np.exp(spread * noise) if base else spread * noise
        out[name] = jnp.asarray(drawn.astype(out[name].dtype))
    for name, factor in factors.items():
        out[name] = (out[name] * factor).astype(out[name].dtype)
    return out
```

```python
from contextlib import ExitStack

import numpy as np
import concourse.bass as bass
from concourse import mybir

F32 = mybir.dt.float32
BF16 = mybir.dt.bfloat16
I32 = mybir.dt.int32
U32 = mybir.dt.uint32
ALU = mybir.AluOpType
ACT = mybir.ActivationFunctionType
AX = mybir.AxisListType

P = 128
NB, NT, F = 32, 256, 128
S = NT // P
TILES = NB * S
TOKENS = NB * NT
H, HD = 16, 8
E, HID = 8, 512
HC = HID // P
REGION = 8448
assert REGION >= TOKENS + P and REGION % 256 == 0
ROW = F + 1
PAD_TOKEN = 1 << 20
FT = TOKENS // P + E
XCH = 4
U1 = 4
U2 = 2
FPB = 2
GR = 4
TCH = 4


def steps(eng, head, full, hi, unroll, body):
    first = head
    whole = full - first
    assert first % unroll == 0 and whole % unroll == 0
    for i in range(first):
        body(i, i % unroll)
    if whole:
        with eng.Fori(0, whole // unroll) as v:
            for k in range(unroll):
                body(v * unroll + (first + k), k)
    for i in range(first + whole, hi):
        body(i, i % unroll)


def block_kernel(nc, x, Wq, bq, Wk, bk, Wv, bv, Wo, bo, m, Wr, W1, W2, out):
    ctx = ExitStack()
    with ctx:
        def sb(name, shape, dt=F32):
            return ctx.enter_context(nc.sbuf_tensor(name, shape, dt))

        def sem(name):
            return ctx.enter_context(nc.semaphore(name))

        x_res = sb("x_res", [P, NB, S * F])
        q_all = sb("q_all", [P, NB, S * F])
        mat_all = sb("mat_all", [P, NB, F])
        qnorm_all = sb("qnorm_all", [P, NB, S * H])
        top8 = sb("top8", [P, U1, S, E])
        w1_sb = sb("w1_sb", [P, E, HID])
        w2_sb = sb("w2_sb", [P, E, HC * F])
        wqk = sb("wqk", [P, 2 * F])
        wvr = sb("wvr", [P, F + E])
        wo = sb("wo", [P, F])
        ident = sb("ident", [P, P])
        head_scale = sb("head_scale", [P, F])
        tri = sb("tri", [P, P], BF16)
        ones = sb("ones", [P, P], BF16)
        region0 = sb("region0", [1, S, E], BF16)
        NBIAS = 2 * F + F + E + F
        bias3 = sb("bias3", [3, NBIAS])
        rest3 = sb("rest3", [3, NBIAS])
        part3 = sb("part3", [3, 3, NBIAS], BF16)
        pick3 = sb("pick3", [3, 3])
        bias_parts = sb("bias_parts", [3, NBIAS], BF16)
        out_bias2 = sb("out_bias2", [3, S, F], BF16)
        expert_no = sb("expert_no", [P, E])
        lane_no = sb("lane_no", [P, 1])
        token_no = sb("token_no", [P, TILES], I32)
        m_row = sb("m_row", [P, H])
        m_work = sb("m_work", [P, 3, H])
        rowi = sb("rowi", [P, 1], I32)
        coli = sb("coli", [P, P], I32)
        rowf = sb("rowf", [P, 1])
        stats = sb("stats", [P, TILES, 6])
        meanvar = sb("meanvar", [P, TILES, 2])
        rstd = sb("rstd", [P, 3, TILES])
        rows = sb("rows", [P, U1, S, ROW])
        xnT = sb("xnT", [P, U1, S * P])
        squares = sb("squares", [P, U1, S * 2 * F])
        sumsq = sb("sumsq", [P, U1, S, 2 * H])
        clamped = sb("clamped", [P, U1, S, 2 * H])
        knorm = sb("knorm", [P, U1, S * H])
        rk = sb("rk", [P, U1, S * H])
        kn = sb("kn", [P, U1, S * F])
        vr = sb("vr", [P, U1, S, F + E])
        kvT = sb("kvT", [P, U1, F])
        topidx = sb("topidx", [P, U1, S, E], U32)
        onehot = sb("onehot", [P, U1, S, E], BF16)
        seen = sb("seen", [P, S, E], BF16)
        prefix1 = sb("prefix1", [P, U1, S, E])
        place = sb("place", [P, U1, S], I32)
        pad_rows = sb("pad_rows", [P, ROW])
        pad_place = sb("pad_place", [P, E], I32)
        list_end = sb("list_end", [P, E])
        te = sb("te", [1, 8, E])
        te_i = sb("te_i", [1, 2, E], I32)
        tile_no = sb("tile_no", [1, FT])
        reached = sb("reached", [1, 2, FT, E])
        tj = sb("tj", [1, 3, FT])
        tile_expert = sb("tile_expert", [1, FT], I32)
        tile_row = sb("tile_row", [1, FT], I32)
        grows = sb("grows", [P, GR, ROW])
        w1_now = sb("w1_now", [P, 2, HID])
        gT = sb("gT", [P, 2, P])
        hT = sb("hT", [P, 2, HID])
        yrows = sb("yrows", [P, GR, F])
        rq = sb("rq", [P, U2, S * H])
        qn = sb("qn", [P, U2, S * F])
        qnT = sb("qnT", [P, U2, S * P])
        wtop = sb("wtop", [P, 4, TILES])

        banks = [ctx.enter_context(nc.psum_tensor(f"bank{i}", [P, 512], F32)) for i in range(8)]
        xT_ps = [banks[0], banks[1]]
        qk_ps = [banks[2], banks[3]]
        vr_ps, kvT_ps, mat_ps, place_ps = banks[4:8]
        qT_ps, o_ps, gT_ps = banks[0], banks[1], banks[2]
        h_ps = [banks[3], banks[4]]
        y_ps = [banks[5], banks[6]]

        rows_dram = nc.dram_tensor("rows_dram", (E * REGION + P, ROW), F32, kind="Internal").ap()
        y_dram = nc.dram_tensor("y_dram", (TOKENS, F), F32, kind="Internal").ap()

        x_loaded = [sem(f"x_loaded{c}") for c in range(NB // XCH)]
        w_loaded = sem("w_loaded")
        bias_loaded = sem("bias_loaded")
        ffn_loaded = sem("ffn_loaded")
        consts_pool = sem("consts_pool")
        consts_dve = sem("consts_dve")
        chain_p = sem("chain_p")
        chain_v = sem("chain_v")
        setup_act = sem("setup_act")
        stats_done = sem("stats_done")
        aggr_done = sem("aggr_done")
        eps_done = sem("eps_done")
        std_ready = sem("std_ready")
        rstd_ready = sem("rstd_ready")
        xn_ready = sem("xn_ready")
        xT_in_psum = sem("xT_in_psum")
        xT_ready = sem("xT_ready")
        qk_in_psum = sem("qk_in_psum")
        vr_in_psum = sem("vr_in_psum")
        q_saved = sem("q_saved")
        squares_ready = sem("squares_ready")
        vr_ready = sem("vr_ready")
        sumsq_ready = sem("sumsq_ready")
        clamped_ready = sem("clamped_ready")
        norms_ready = sem("norms_ready")
        rk_ready = sem("rk_ready")
        kn_ready = sem("kn_ready")
        top_ready = sem("top_ready")
        topidx_ready = sem("topidx_ready")
        onehot_ready = sem("onehot_ready")
        seen_ready = sem("seen_ready")
        prefix_in_psum = sem("prefix_in_psum")
        prefix1_ready = sem("prefix1_ready")
        place_ready = sem("place_ready")
        token_written = sem("token_written")
        scattered = [sem(f"scattered{r}") for r in range(U1)]
        kvT_in_psum = sem("kvT_in_psum")
        kvT_ready = sem("kvT_ready")
        mat_in_psum = sem("mat_in_psum")
        mat_ready = sem("mat_ready")
        ends_in_psum = sem("ends_in_psum")
        ends_ready = sem("ends_ready")
        pads_scattered = sem("pads_scattered")
        spare_written = sem("spare_written")
        table_ready = sem("table_ready")
        g_loaded = [sem(f"g_loaded{r}") for r in range(GR)]
        w1_staged = sem("w1_staged")
        gT_in_psum = sem("gT_in_psum")
        gT_ready = sem("gT_ready")
        h_in_psum = sem("h_in_psum")
        hT_ready = sem("hT_ready")
        y_in_psum = sem("y_in_psum")
        y_ready = sem("y_ready")
        y_stored = [sem(f"y_stored{r}") for r in range(GR)]
        rq_ready = sem("rq_ready")
        qn_ready = sem("qn_ready")
        qT_in_psum = sem("qT_in_psum")
        qT_ready = sem("qT_ready")
        o_in_psum = sem("o_in_psum")
        res_ready = sem("res_ready")
        gap_ready = sem("gap_ready")
        exp_ready = sem("exp_ready")
        wtop_ready = sem("wtop_ready")
        y_loaded = [sem(f"y_loaded{c}") for c in range(NB // TCH)]
        final_ready = sem("final_ready")
        out_stored = sem("out_stored")

        x_dram = x.rearrange("b (p s) f -> p b (s f)", s=S)
        out_dram = out.rearrange("b (p s) f -> p b (s f)", s=S)
        yb_dram = y_dram.rearrange("(b p s) f -> p b (s f)", p=P, s=S)

        def heads(ap):
            return ap.rearrange("p (g d) -> p g d", d=HD)

        def spread(ap, shape):
            return ap.unsqueeze(2).broadcast_to(shape)

        def wait(eng, s, n):
            if not (isinstance(n, int) and n <= 0):
                eng.wait_ge(s, n)

        def stage(i, c_lag, fn, r, depth):
            if isinstance(i, int) and not 0 <= i - c_lag < NB:
                return
            fn(i - c_lag, (r - c_lag) % depth)

        STEPS1 = NB + 4
        FSTEPS = FT // FPB
        ctx.enter_context(nc.allow_low_precision(reason="row numbers are integers below 2^24"))
        block = ctx.enter_context(nc.Block())

        @block.sync
        def _(sp):
            for c in range(NB // XCH):
                b = slice(c * XCH, (c + 1) * XCH)
                sp.dma_start(x_res[:, b, :], x_dram[:, b, :]).then_inc(x_loaded[c], 16)
            sp.dma_start(w1_sb[:], W1.rearrange("e d h -> d e h")).then_inc(ffn_loaded, 16)
            sp.dma_start(w2_sb[:].rearrange("p e (c d) -> p e c d", c=HC),
                         W2.rearrange("e (c p) d -> p e c d", p=P)).then_inc(ffn_loaded, 16)
            sp.wait_ge(consts_pool, 1)
            sp.dma_start(rows_dram[E * REGION:E * REGION + P, :], pad_rows[:]).then_inc(spare_written, 16)
            sp.wait_ge(spare_written, 16)

            sp.wait_ge(table_ready, 1)
            for r in range(U1):
                sp.wait_ge(scattered[r], 32 * (NB // U1))
            sp.wait_ge(pads_scattered, 16 * E)

            def load_rows(j, r):
                wait(sp, gT_in_psum, j - GR + 1)
                if not (isinstance(j, int) and j < GR):
                    sp.wait_ge(y_stored[r], (j - r) // GR * 16)
                row = sp.value_load(tile_row[0:1, bass.ds(j, 1)], min_val=0, max_val=E * REGION)
                sp.dma_start(grows[:, r, :], rows_dram[bass.ds(row, P), :]).then_inc(g_loaded[r], 16)

            steps(sp, GR, FT, FT, GR, load_rows)

            for r in range(GR):
                sp.wait_ge(y_stored[r], 16 * (FT // GR))
            sp.wait_ge(qn_ready, NB)
            for c in range(NB // TCH):
                b = slice(c * TCH, (c + 1) * TCH)
                sp.dma_start(q_all[:, b, :], yb_dram[:, b, :]).then_inc(y_loaded[c], 16)
            for c in range(NB // TCH):
                b = slice(c * TCH, (c + 1) * TCH)
                sp.wait_ge(final_ready, c + 1)
                sp.dma_start(out_dram[:, b, :], x_res[:, b, :]).then_inc(out_stored, 16)
            sp.wait_ge(out_stored, 16 * (NB // TCH))

        @block.gpsimd
        def _(pool):
            nc.gpsimd.memset(pad_rows[:, 0:F], 0.0)
            nc.gpsimd.memset(pad_rows[:, F:ROW].bitcast(I32), PAD_TOKEN).then_inc(consts_pool, 1)
            nc.gpsimd.memset(ident[:], 0.0).then_inc(chain_p, 1)
            nc.gpsimd.memset(tri[:], 1.0).then_inc(chain_p, 1)
            nc.gpsimd.memset(ones[:], 1.0)
            nc.gpsimd.memset(seen[:], 0.0)
            nc.gpsimd.memset(pick3[:], 0.0).then_inc(chain_p, 1)
            nc.gpsimd.iota(region0[0:1], [[0, S], [REGION, E]], base=0, channel_multiplier=0,
                           allow_small_or_imprecise_dtypes=True)
            nc.gpsimd.iota(expert_no[:], [[1, E]], base=0, channel_multiplier=0,
                           allow_small_or_imprecise_dtypes=True)
            nc.gpsimd.iota(lane_no[:], [[0, 1]], base=0, channel_multiplier=1,
                           allow_small_or_imprecise_dtypes=True)
            nc.gpsimd.iota(tile_no[0:1, :], [[1, FT]], base=0, channel_multiplier=0,
                           allow_small_or_imprecise_dtypes=True)
            nc.gpsimd.iota(token_no[:], [[NT, NB], [1, S]], base=0, channel_multiplier=S)
            nc.gpsimd.iota(rowi[:], [[0, 1]], base=0, channel_multiplier=1)
            nc.gpsimd.iota(coli[:], [[1, P]], base=0, channel_multiplier=0).then_inc(consts_pool, 1)
            pool.wait_ge(chain_p, 3)
            nc.gpsimd.affine_select(out=ident[:], in_=ident[:], compare_op=ALU.not_equal, fill=1.0, base=0,
                                    pattern=[[-1, P]], channel_multiplier=1)
            nc.gpsimd.affine_select(out=tri[:], in_=tri[:], compare_op=ALU.is_gt, fill=0.0, base=0,
                                    pattern=[[1, P]], channel_multiplier=-1)
            nc.gpsimd.affine_select(out=pick3[:], in_=pick3[:], compare_op=ALU.not_equal, fill=1.0, base=0,
                                    pattern=[[-1, 3]], channel_multiplier=1).then_inc(consts_pool, 1)

            pool.wait_ge(consts_pool, 3)
            def token_col(c, r):
                if not (isinstance(c, int) and c < U1):
                    pool.wait_ge(scattered[r], (c - r) // U1 * 32)
                nc.gpsimd.tensor_copy(rows[:, r, :, F].bitcast(I32),
                                      token_no[:, bass.ds(c * S, S)]).then_inc(token_written, 1)

            def logit_gap(c, r):
                pool.wait_ge(top_ready, c + 1)
                nc.gpsimd.tensor_tensor(wtop[:, 0, bass.ds(c * S, S)], top8[:, r, :, 1], top8[:, r, :, 0],
                                        ALU.subtract).then_inc(gap_ready, 1)

            def scatter(c, r):
                pool.wait_ge(consts_pool, 3)
                pool.wait_ge(token_written, c + 1)
                pool.wait_ge(xn_ready, c + 1)
                pool.wait_ge(place_ready, c + 1)
                for s in range(S):
                    nc.gpsimd.indirect_dma_start(
                        rows_dram, bass.IndirectOffsetOnAxis(ap=place[:, r, s:s + 1], axis=0),
                        rows[:, r, s, :], None).then_inc(scattered[r], 16)

            def step1(i, r):
                stage(i, 0, token_col, r, U1)
                stage(i, 2, logit_gap, r, U1)
                stage(i, 2, scatter, r, U1)

            steps(pool, 2 * U1, NB, NB + 2, U1, step1)

            pool.wait_ge(ends_ready, 2)
            for e in range(E):
                nc.gpsimd.indirect_dma_start(
                    rows_dram, bass.IndirectOffsetOnAxis(ap=pad_place[:, e:e + 1], axis=0),
                    pad_rows[:], None).then_inc(pads_scattered, 16)

            pool.wait_ge(table_ready, 1)
            pool.wait_ge(ffn_loaded, 32)

            def stage_w1(j, r):
                e = pool.value_load(tile_expert[0:1, bass.ds(j, 1)], min_val=0, max_val=E - 1)
                wait(pool, h_in_psum, j - 1)
                nc.gpsimd.tensor_copy(w1_now[:, r % 2, :],
                                      w1_sb[:, bass.ds(e, 1), :].rearrange("p a h -> p (a h)")).then_inc(w1_staged, 1)

            def store_y(j, r):
                pool.wait_ge(consts_pool, 3)
                pool.wait_ge(y_ready, j + 1)
                nc.gpsimd.indirect_dma_start(
                    y_dram, bass.IndirectOffsetOnAxis(ap=grows[:, r, F:ROW].bitcast(I32), axis=0),
                    yrows[:, r, :], None, bounds_check=TOKENS - 1, oob_is_err=False).then_inc(y_stored[r], 16)

            def qn_of(c, r):
                pool.wait_ge(rq_ready, c + 1)
                wait(pool, qT_in_psum, c - U2 + 1)
                nc.gpsimd.tensor_tensor(
                    heads(qn[:, r, :]), heads(q_all[:, bass.ds(c, 1), :].rearrange("p a f -> p (a f)")),
                    spread(rq[:, r, :], [P, S * H, HD]), ALU.mult).then_inc(qn_ready, 1)

            def step2(i, r):
                stage(i, 0, qn_of, r, U2)
                for t in range(FPB):
                    rr = r * FPB + t
                    stage_w1(i * FPB + t, rr)
                    if not (isinstance(i, int) and i * FPB + t < 2):
                        store_y(i * FPB + t - 2, (rr - 2) % GR)

            steps(pool, U2, NB, FSTEPS, U2, step2)
            for j in range(FT - 2, FT):
                store_y(j, j % GR)

        @block.scalar
        def _(act):
            for dst, src in ((wqk[:, 0:F], Wq), (wqk[:, F:2 * F], Wk), (wvr[:, 0:F], Wv), (wvr[:, F:F + E], Wr),
                             (wo[:], Wo)):
                act.dma_start(dst, src).then_inc(w_loaded, 16)
            for n, b in enumerate((bq, bk, bv)):
                act.dma_start(bias3[:, n * F:(n + 1) * F], b.partition_broadcast(3)).then_inc(bias_loaded, 16)
            act.dma_start(bias3[:, NBIAS - F:NBIAS], bo.partition_broadcast(3)).then_inc(bias_loaded, 16)
            act.dma_start(m_row[:], m.partition_broadcast(P)).then_inc(bias_loaded, 16)
            act.wait_ge(bias_loaded, 16 * 5)
            nc.scalar.activation(m_work[:, 0, :], m_row[:], ACT.Exp, scale=-1.0).then_inc(setup_act, 1)
            act.wait_ge(consts_dve, 1)
            nc.scalar.activation(m_work[:, 2, :], m_work[:, 1, :], ACT.Exp,
                                 scale=-float(np.log(NT))).then_inc(setup_act, 1)
            act.wait_ge(eps_done, 1)
            nc.scalar.activation(rstd[:, 1, :], rstd[:, 0, :], ACT.Sqrt).then_inc(std_ready, 1)

            def xT_copy(c, r):
                act.wait_ge(xT_in_psum, c + 1)
                wait(act, vr_in_psum, c - U1 + 1)
                nc.scalar.copy(xnT[:, r, :], xT_ps[r % 2][:, 0:S * P]).then_inc(xT_ready, 1)

            def take_qk(c, r):
                act.wait_ge(qk_in_psum, c + 1)
                qk = qk_ps[r % 2][:].rearrange("p (s f) -> p s f", s=S)
                nc.scalar.copy(q_all[:, bass.ds(c, 1), :].rearrange("p a (s f) -> p (a s) f", s=S),
                               qk[:, :, 0:F]).then_inc(q_saved, 1)
                wait(act, sumsq_ready, c - U1 + 1)
                nc.scalar.activation(squares[:, r, :], qk_ps[r % 2][:], ACT.Square).then_inc(squares_ready, 1)

            def take_vr(c, r):
                act.wait_ge(vr_in_psum, c + 1)
                wait(act, kvT_in_psum, c - U1 + 1)
                wait(act, topidx_ready, c - U1 + 1)
                nc.scalar.copy(vr[:, r], vr_ps[:, 0:S * (F + E)].rearrange("p (s f) -> p s f", s=S)
                               ).then_inc(vr_ready, 1)

            def norms(c, r):
                act.wait_ge(clamped_ready, c + 1)
                wait(act, rk_ready, c - U1 + 1)
                nc.scalar.activation(qnorm_all[:, bass.ds(c, 1), :].rearrange("p a (s h) -> p (a s) h", s=S),
                                     clamped[:, r, :, 0:H], ACT.Sqrt)
                nc.scalar.activation(knorm[:, r, :].rearrange("p (s h) -> p s h", s=S),
                                     clamped[:, r, :, H:2 * H], ACT.Sqrt).then_inc(norms_ready, 1)

            def mat_copy(c, r):
                act.wait_ge(mat_in_psum, c + 1)
                nc.scalar.copy(mat_all[:, bass.ds(c, 1), :].rearrange("p a f -> p (a f)"),
                               mat_ps[:, 0:F]).then_inc(mat_ready, 1)

            def step1(i, r):
                stage(i, 0, xT_copy, r, U1)
                stage(i, 2, norms, r, U1)
                stage(i, 1, take_qk, r, U1)
                stage(i, 1, take_vr, r, U1)
                stage(i, 4, mat_copy, r, U1)

            steps(act, 2 * U1, NB, STEPS1, U1, step1)

            def gelu(j, r):
                act.wait_ge(h_in_psum, j + 1)
                wait(act, y_in_psum, j - 1)
                nc.scalar.activation(hT[:, r % 2, :], h_ps[r % 2][:], ACT.Gelu).then_inc(hT_ready, 1)

            def qT_copy(c, r):
                act.wait_ge(qT_in_psum, c + 1)
                wait(act, o_in_psum, c - U2 + 1)
                nc.scalar.copy(qnT[:, r, :], qT_ps[:, 0:S * P]).then_inc(qT_ready, 1)

            def step2(i, r):
                gelu(i * FPB, r * FPB)
                stage(i, 0, qT_copy, r, U2)
                gelu(i * FPB + 1, r * FPB + 1)

            steps(act, U2, NB, FSTEPS, U2, step2)
            act.wait_ge(gap_ready, NB)
            nc.scalar.activation(wtop[:, 1, :], wtop[:, 0, :], ACT.Exp).then_inc(exp_ready, 1)

        @block.vector
        def _(dve):
            links = [0]

            def link(ins):
                links[0] += 1
                ins.then_inc(chain_v, 1)
                dve.wait_ge(chain_v, links[0])

            V = nc.vector
            dve.wait_ge(consts_pool, 3)
            link(V.memset(bias3[:, 3 * F:3 * F + E], 0.0))
            dve.wait_ge(bias_loaded, 16 * 5)
            link(V.tensor_copy(part3[:, 0, :], bias3[:]))
            link(V.tensor_tensor(rest3[:], bias3[:], part3[:, 0, :], ALU.subtract))
            link(V.tensor_copy(part3[:, 1, :], rest3[:]))
            link(V.tensor_tensor(rest3[:], rest3[:], part3[:, 1, :], ALU.subtract))
            link(V.tensor_copy(part3[:, 2, :], rest3[:]))
            link(V.tensor_scalar(bias_parts[:], part3[:, 0, :], pick3[:, 0:1], None, ALU.mult))
            for n in (1, 2):
                link(V.scalar_tensor_tensor(out=bias_parts[:], in0=part3[:, n, :], scalar=pick3[:, n:n + 1],
                                            in1=bias_parts[:], op0=ALU.mult, op1=ALU.add))
            V.tensor_copy(out_bias2[:], bias_parts[:, NBIAS - F:NBIAS].unsqueeze(1).broadcast_to([3, S, F]))
            dve.wait_ge(setup_act, 1)
            link(V.tensor_scalar(m_work[:, 1, :], m_work[:, 0, :], 1.0, None, ALU.add))
            V.reciprocal(m_work[:, 1, :], m_work[:, 1, :]).then_inc(consts_dve, 1)
            link(V.tensor_scalar(rowi[:], rowi[:], 3, None, ALU.arith_shift_right))
            link(V.tensor_scalar(coli[:], coli[:], 3, None, ALU.arith_shift_right))
            link(V.tensor_copy(rowf[:], rowi[:]))
            link(V.tensor_scalar(head_scale[:], coli[:], rowf[:, 0:1], None, ALU.is_equal))
            dve.wait_ge(setup_act, 2)
            V.tensor_tensor(heads(head_scale[:]), heads(head_scale[:]), spread(m_work[:, 2, :], [P, H, HD]),
                            ALU.mult).then_inc(consts_dve, 1)

            TPC = XCH * S
            for c in range(NB // XCH):
                dve.wait_ge(x_loaded[c], 16)
                for t in range(c * TPC, (c + 1) * TPC):
                    ins = V.bn_stats(stats[:, t, :], x_res[:, t // S, (t % S) * F:(t % S + 1) * F])
                ins.then_inc(stats_done, 1)
                dve.wait_ge(stats_done, c + 1)
                for t in range(c * TPC, (c + 1) * TPC):
                    ins = V.bn_aggr(meanvar[:, t, :], stats[:, t, :])
            ins.then_inc(aggr_done, 1)
            dve.wait_ge(aggr_done, 1)
            V.tensor_scalar(rstd[:, 0, :], meanvar[:, :, 1], 1e-5, None, ALU.add).then_inc(eps_done, 1)
            dve.wait_ge(std_ready, 1)
            V.reciprocal(rstd[:, 2, :], rstd[:, 1, :]).then_inc(rstd_ready, 1)
            dve.wait_ge(rstd_ready, 1)

            def normalise(c, r):
                wait(dve, xT_in_psum, c - U1 + 1)
                if not (isinstance(c, int) and c < U1):
                    dve.wait_ge(scattered[r], (c - r) // U1 * 32)
                for s in range(S):
                    ins = V.tensor_scalar(
                        rows[:, r, s, 0:F], x_res[:, bass.ds(c, 1), s * F:(s + 1) * F].rearrange("p a f -> p (a f)"),
                        meanvar[:, bass.ds(c * S + s, 1), 0], rstd[:, 2, bass.ds(c * S + s, 1)],
                        ALU.subtract, ALU.mult)
                ins.then_inc(xn_ready, 1)

            def sum_squares(c, r):
                dve.wait_ge(squares_ready, c + 1)
                wait(dve, clamped_ready, c - U1 + 1)
                V.tensor_reduce(sumsq[:, r].rearrange("p s h -> p (s h)"), heads(squares[:, r, :]), AX.X,
                                ALU.add).then_inc(sumsq_ready, 1)

            def clamp(c, r):
                dve.wait_ge(sumsq_ready, c + 1)
                wait(dve, norms_ready, c - U1 + 1)
                V.tensor_scalar(clamped[:, r], sumsq[:, r], 1e-24, None, ALU.max).then_inc(clamped_ready, 1)

            def top(c, r):
                dve.wait_ge(consts_pool, 3)
                dve.wait_ge(vr_ready, c + 1)
                wait(dve, gap_ready, c - U1 + 1)
                for s in range(S):
                    ins = V.max(top8[:, r, s, :], vr[:, r, s, F:F + E])
                ins.then_inc(top_ready, 1)

            def top_index(c, r):
                dve.wait_ge(consts_pool, 3)
                dve.wait_ge(top_ready, c + 1)
                wait(dve, onehot_ready, c - U1 + 1)
                for s in range(S):
                    ins = V.max_index(topidx[:, r, s, :], top8[:, r, s, :],
                                      vr[:, r, s, F:F + E])
                ins.then_inc(topidx_ready, 1)

            def one_hot(c, r):
                dve.wait_ge(topidx_ready, c + 1)
                wait(dve, prefix_in_psum, c - U1 + 1)
                V.tensor_tensor(onehot[:, r], expert_no[:].unsqueeze(1).broadcast_to([P, S, E]),
                                topidx[:, r, :, 0:1].broadcast_to([P, S, E]), ALU.is_equal).then_inc(onehot_ready, 1)

            def mask_prefix(c, r):
                dve.wait_ge(prefix_in_psum, c + 1)
                V.tensor_tensor(prefix1[:, r], place_ps[:, 0:S * E].rearrange("p (s e) -> p s e", s=S),
                                onehot[:, r], ALU.mult).then_inc(prefix1_ready, 1)
                wait(dve, seen_ready, c)
                V.tensor_tensor(seen[:], seen[:], onehot[:, r], ALU.add).then_inc(seen_ready, 1)

            def find_place(c, r):
                dve.wait_ge(prefix1_ready, c + 1)
                if not (isinstance(c, int) and c < U1):
                    dve.wait_ge(scattered[r], (c - r) // U1 * 32)
                V.tensor_reduce(place[:, r, :], prefix1[:, r], AX.X, ALU.add).then_inc(place_ready, 1)

            def recip_k(c, r):
                dve.wait_ge(norms_ready, c + 1)
                wait(dve, kn_ready, c - U1 + 1)
                V.reciprocal(rk[:, r, :], knorm[:, r, :]).then_inc(rk_ready, 1)

            def scale_k(c, r):
                dve.wait_ge(rk_ready, c + 1)
                dve.wait_ge(squares_ready, c + 1)
                wait(dve, kvT_in_psum, c - U1 + 1)
                for s in range(S):
                    ins = V.tensor_tensor(heads(kn[:, r, s * F:(s + 1) * F]),
                                          heads(qk_ps[r % 2][:, s * 2 * F + F:(s + 1) * 2 * F]),
                                          spread(rk[:, r, s * H:(s + 1) * H], [P, H, HD]), ALU.mult)
                ins.then_inc(kn_ready, 1)

            def mask_kvT(c, r):
                dve.wait_ge(kvT_in_psum, c + 1)
                wait(dve, mat_in_psum, c - U1 + 1)
                V.tensor_tensor(kvT[:, r, :], kvT_ps[:, 0:F], head_scale[:], ALU.mult).then_inc(kvT_ready, 1)

            dve.wait_ge(consts_dve, 2)

            def step1(i, r):
                stage(i, 0, normalise, r, U1)
                stage(i, 2, mask_prefix, r, U1)
                stage(i, 2, recip_k, r, U1)
                stage(i, 2, find_place, r, U1)
                stage(i, 2, scale_k, r, U1)
                stage(i, 1, top, r, U1)
                stage(i, 3, mask_kvT, r, U1)
                stage(i, 1, top_index, r, U1)
                stage(i, 1, sum_squares, r, U1)
                stage(i, 1, one_hot, r, U1)
                stage(i, 1, clamp, r, U1)

            steps(dve, 2 * U1, NB, STEPS1, U1, step1)

            dve.wait_ge(ends_in_psum, 1)
            V.tensor_copy(list_end[:], place_ps[:, 0:E]).then_inc(ends_ready, 1)
            dve.wait_ge(ends_ready, 1)
            V.tensor_scalar(pad_place[:], list_end[:], lane_no[:, 0:1], None, ALU.add).then_inc(ends_ready, 1)
            link(V.tensor_tensor(te[0:1, 0, :], list_end[0:1, :], region0[0:1, 0, :], ALU.subtract))
            link(V.tensor_scalar(te_i[0:1, 0, :], te[0:1, 0, :], float(P - 1), None, ALU.add))
            link(V.tensor_scalar(te_i[0:1, 1, :], te_i[0:1, 0, :], 7, None, ALU.arith_shift_right))
            link(V.tensor_copy(te[0:1, 1, :], te_i[0:1, 1, :]))
            link(V.memset(te[0:1, 2, :], 1.0))
            link(V.tensor_tensor_scan(te[0:1, 3, :], te[0:1, 2, :], te[0:1, 1, :], 0.0, ALU.mult, ALU.add))
            link(V.tensor_scalar(te[0:1, 4, :], te[0:1, 1, :], -float(P), float(REGION), ALU.mult, ALU.add))
            link(V.tensor_tensor(reached[0:1, 0], tile_no[0:1, :].unsqueeze(2).broadcast_to([1, FT, E]),
                                 te[0:1, 3, :].unsqueeze(1).broadcast_to([1, FT, E]), ALU.is_ge))
            link(V.tensor_reduce(tj[0:1, 0, :], reached[0:1, 0], AX.X, ALU.add))
            link(V.tensor_tensor(reached[0:1, 1], reached[0:1, 0],
                                 te[0:1, 4, :].unsqueeze(1).broadcast_to([1, FT, E]), ALU.mult))
            link(V.tensor_reduce(tj[0:1, 1, :], reached[0:1, 1], AX.X, ALU.add))
            link(V.scalar_tensor_tensor(out=tj[0:1, 2, :], in0=tile_no[0:1, :], scalar=float(P),
                                        in1=tj[0:1, 1, :], op0=ALU.mult, op1=ALU.add))
            link(V.tensor_scalar(tile_expert[0:1, :], tj[0:1, 0, :], float(E - 1), None, ALU.min))
            V.tensor_scalar(tile_row[0:1, :], tj[0:1, 2, :], float(E * REGION), None, ALU.min).then_inc(table_ready, 1)

            def gT_copy(j, r):
                dve.wait_ge(gT_in_psum, j + 1)
                wait(dve, h_in_psum, j - 1)
                V.tensor_copy(gT[:, r % 2, :], gT_ps[:, 0:P]).then_inc(gT_ready, 1)

            def y_copy(j, r):
                dve.wait_ge(y_in_psum, j + 1)
                if not (isinstance(j, int) and j < GR):
                    dve.wait_ge(y_stored[r], (j - r) // GR * 16)
                V.tensor_copy(yrows[:, r, :], y_ps[r % 2][:, 0:F]).then_inc(y_ready, 1)

            def recip_q(c, r):
                wait(dve, qn_ready, c - U2 + 1)
                V.reciprocal(rq[:, r, :], qnorm_all[:, bass.ds(c, 1), :].rearrange("p a h -> p (a h)")
                             ).then_inc(rq_ready, 1)

            def add_attention(c, r):
                dve.wait_ge(o_in_psum, c + 1)
                xb = x_res[:, bass.ds(c, 1), :].rearrange("p a f -> p (a f)")
                V.tensor_tensor(xb, xb, o_ps[:, 0:S * F], ALU.add).then_inc(res_ready, 1)

            dve.wait_ge(norms_ready, NB)

            def step2(i, r):
                for t in range(FPB):
                    j = i * FPB + t
                    gT_copy(j, r * FPB + t)
                    if t == 0:
                        stage(i, -1, recip_q, r, U2)
                    if t == 1:
                        stage(i, 1, add_attention, r, U2)
                    if not (isinstance(j, int) and j < 2):
                        y_copy(j - 2, (r * FPB + t - 2) % GR)

            recip_q(0, 0)
            steps(dve, U2, NB - U2, FSTEPS, U2, step2)
            for j in range(FT - 2, FT):
                y_copy(j, j % GR)
            dve.wait_ge(exp_ready, 1)
            V.tensor_scalar(wtop[:, 2, :], wtop[:, 1, :], 1.0, None, ALU.add).then_inc(wtop_ready, 1)
            dve.wait_ge(wtop_ready, 1)
            V.reciprocal(wtop[:, 3, :], wtop[:, 2, :]).then_inc(wtop_ready, 1)
            dve.wait_ge(wtop_ready, 2)
            dve.wait_ge(res_ready, NB)
            for c in range(NB // TCH):
                dve.wait_ge(y_loaded[c], 16)
                for t in range(c * TCH * S, (c + 1) * TCH * S):
                    f = slice((t % S) * F, (t % S + 1) * F)
                    ins = V.scalar_tensor_tensor(out=x_res[:, t // S, f], in0=q_all[:, t // S, f],
                                                 scalar=wtop[:, 3, t:t + 1], in1=x_res[:, t // S, f],
                                                 op0=ALU.mult, op1=ALU.add)
                ins.then_inc(final_ready, 1)

        @block.tensor
        def _(pe):
            T = nc.tensor
            pe.wait_ge(w_loaded, 16 * 5)
            pe.wait_ge(consts_pool, 3)
            pe.wait_ge(consts_dve, 2)

            def transposes(c, r):
                pe.wait_ge(xn_ready, c + 1)
                wait(pe, xT_ready, c - 1)
                for s in range(S):
                    ins = T.transpose(xT_ps[r % 2][:, s * P:(s + 1) * P], rows[:, r, s, 0:F], ident[:])
                ins.then_inc(xT_in_psum, 1)

            def project(c, r):
                pe.wait_ge(xT_ready, c + 1)
                wait(pe, kn_ready, c - 1)
                wait(pe, q_saved, c - 1)
                for s in range(S):
                    o = qk_ps[r % 2][:, s * 2 * F:(s + 1) * 2 * F]
                    T.matmul(o, ones[0:3, :], bias_parts[:, 0:2 * F], start=True, stop=False)
                    ins = T.matmul(o, xnT[:, r, s * P:(s + 1) * P], wqk[:], start=False, stop=True)
                ins.then_inc(qk_in_psum, 1)
                wait(pe, vr_ready, c)
                for s in range(S):
                    o = vr_ps[:, s * (F + E):(s + 1) * (F + E)]
                    T.matmul(o, ones[0:3, :], bias_parts[:, 2 * F:3 * F + E], start=True, stop=False)
                    ins = T.matmul(o, xnT[:, r, s * P:(s + 1) * P], wvr[:], start=False, stop=True)
                ins.then_inc(vr_in_psum, 1)

            def prefix_base():
                T.matmul(place_ps[:, 0:S * E], ones[0:1, :], region0[0:1], start=True, stop=False)
                for s in range(S):
                    ins = T.matmul(place_ps[:, 0:S * E], ones[:], seen[:, s:s + 1, :].broadcast_to([P, S, E]),
                                   start=False, stop=False)
                return ins

            def prefixes(c, r):
                pe.wait_ge(onehot_ready, c + 1)
                wait(pe, seen_ready, c)
                wait(pe, prefix1_ready, c)
                prefix_base()
                T.matmul(place_ps[:, E:2 * E], ones[:], onehot[:, r, 0, :], start=False, stop=False)
                T.matmul(place_ps[:, 0:S * E], tri[:], onehot[:, r], start=False, stop=True
                         ).then_inc(prefix_in_psum, 1)

            def kv_product(c, r):
                pe.wait_ge(kn_ready, c + 1)
                pe.wait_ge(vr_ready, c + 1)
                wait(pe, kvT_ready, c)
                for s in range(S):
                    ins = T.matmul(kvT_ps[:, 0:F], vr[:, r, s, 0:F], kn[:, r, s * F:(s + 1) * F],
                                   start=(s == 0), stop=(s == S - 1))
                ins.then_inc(kvT_in_psum, 1)

            def with_wo(c, r):
                pe.wait_ge(kvT_ready, c + 1)
                wait(pe, mat_ready, c)
                T.matmul(mat_ps[:, 0:F], kvT[:, r, :], wo[:], start=True, stop=True).then_inc(mat_in_psum, 1)

            def step1(i, r):
                stage(i, 0, transposes, r, U1)
                stage(i, 2, prefixes, r, U1)
                stage(i, 1, project, r, U1)
                stage(i, 3, kv_product, r, U1)
                stage(i, 4, with_wo, r, U1)

            steps(pe, 2 * U1, NB, STEPS1, U1, step1)
            pe.wait_ge(seen_ready, NB)
            pe.wait_ge(prefix1_ready, NB)
            T.matmul(place_ps[:, 0:S * E], ones[0:1, :], region0[0:1], start=True, stop=False)
            for s in range(S):
                ins = T.matmul(place_ps[:, 0:S * E], ones[:], seen[:, s:s + 1, :].broadcast_to([P, S, E]),
                               start=False, stop=(s == S - 1))
            ins.then_inc(ends_in_psum, 1)

            pe.wait_ge(mat_ready, NB)
            pe.wait_ge(vr_ready, NB)
            pe.wait_ge(kn_ready, NB)
            pe.wait_ge(kvT_ready, NB)
            pe.wait_ge(table_ready, 1)
            pe.wait_ge(ffn_loaded, 32)

            def g_transpose(j, r):
                pe.wait_ge(g_loaded[r], (j - r) // GR * 16 + 16)
                wait(pe, gT_ready, j)
                T.transpose(gT_ps[:, 0:P], grows[:, r, 0:F], ident[:]).then_inc(gT_in_psum, 1)

            def up(j, r):
                pe.wait_ge(gT_ready, j + 1)
                pe.wait_ge(w1_staged, j + 1)
                wait(pe, hT_ready, j - 1)
                for n in range(HC):
                    ins = T.matmul(h_ps[r % 2][:, n * P:(n + 1) * P], w1_now[:, r % 2, n * P:(n + 1) * P],
                                   gT[:, r % 2, :], start=True, stop=True)
                ins.then_inc(h_in_psum, 1)

            def down(j, r):
                e = pe.value_load(tile_expert[0:1, bass.ds(j, 1)], min_val=0, max_val=E - 1)
                pe.wait_ge(hT_ready, j + 1)
                wait(pe, y_ready, j - 1)
                for n in range(HC):
                    ins = T.matmul(y_ps[r % 2][:, 0:F], hT[:, r % 2, n * P:(n + 1) * P],
                                   w2_sb[:, bass.ds(e, 1), n * F:(n + 1) * F].rearrange("p a f -> p (a f)"),
                                   start=(n == 0), stop=(n == HC - 1))
                ins.then_inc(y_in_psum, 1)

            def q_transposes(c, r):
                pe.wait_ge(qn_ready, c + 1)
                wait(pe, qT_ready, c)
                for s in range(S):
                    ins = T.transpose(qT_ps[:, s * P:(s + 1) * P], qn[:, r, s * F:(s + 1) * F], ident[:])
                ins.then_inc(qT_in_psum, 1)

            def attend(c, r):
                pe.wait_ge(qT_ready, c + 1)
                wait(pe, res_ready, c)
                T.matmul(o_ps[:, 0:S * F], ones[0:3, :], out_bias2[:].rearrange("p s f -> p (s f)"),
                         start=True, stop=False)
                for s in range(S):
                    ins = T.matmul(o_ps[:, s * F:(s + 1) * F], qnT[:, r, s * P:(s + 1) * P],
                                   mat_all[:, bass.ds(c, 1), :].rearrange("p a f -> p (a f)"),
                                   start=False, stop=(s == S - 1))
                ins.then_inc(o_in_psum, 1)

            def step2(i, r):
                for t in range(FPB):
                    j, rr = i * FPB + t, r * FPB + t
                    if not (isinstance(j, int) and j + 1 >= FT):
                        g_transpose(j + 1, (rr + 1) % GR)
                    up(j, rr)
                    if t == 0:
                        stage(i, 1, attend, r, U2)
                        stage(i, 0, q_transposes, r, U2)
                    if not (isinstance(j, int) and j < 1):
                        down(j - 1, (rr - 1) % GR)

            g_transpose(0, 0)
            steps(pe, U2, NB, FSTEPS, U2, step2)
            down(FT - 1, (FT - 1) % GR)


_INS = ["L0_attn_x", "L0_attn_Wq", "L0_attn_bq", "L0_attn_Wk", "L0_attn_bk", "L0_attn_Wv", "L0_attn_bv",
        "L0_attn_Wo", "L0_attn_bo", "L0_attn_m", "L0_ffn_Wr", "L0_ffn_W1", "L0_ffn_W2"]
_OUTS = [((NB, NT, F), "float32")]


def kernel(**inputs):
    import numpy as _np
    import concourse.bacc as _bacc
    from concourse import mybir as _mybir
    from concourse.bass_utils import run_bass_kernel_spmd as _run

    nc = _bacc.Bacc("TRN2", target_bir_lowering=False, num_devices=1)
    arrays, args = {}, []
    for name in _INS:
        a = _np.ascontiguousarray(inputs[name])
        arrays[f"in_{name}_dram"] = a
        args.append(nc.dram_tensor(f"in_{name}_dram", a.shape, _mybir.dt.from_np(a.dtype), kind="ExternalInput").ap())
    for i, (shape, dtype) in enumerate(_OUTS):
        dt = _mybir.dt.from_np(_np.dtype(dtype))
        args.append(nc.dram_tensor(f"out_{i}_dram", shape, dt, kind="ExternalOutput").ap())
    block_kernel(nc, *args)
    r = _run(nc, [arrays], core_ids=[0])
    got = tuple(r.results[0][f"out_{i}_dram"] for i in range(len(_OUTS)))
    return got[0]
```

```python
from contextlib import ExitStack

import numpy as np
import concourse.bass as bass
from concourse import mybir

F32 = mybir.dt.float32
BF16 = mybir.dt.bfloat16
I32 = mybir.dt.int32
U32 = mybir.dt.uint32
ALU = mybir.AluOpType
ACT = mybir.ActivationFunctionType
AX = mybir.AxisListType

P = 128
NB, NT, F = 32, 256, 128
S = NT // P
TILES = NB * S
TOKENS = NB * NT
H, HD = 16, 8
E, HID = 8, 512
HC = HID // P
REGION = 8448
assert REGION >= TOKENS + P and REGION % 256 == 0
TOK, GAP = 2 * F, 2 * F + 1
ROW = 2 * F + 2
PAD_TOKEN = float(1 << 20)
FT = TOKENS // P + E
XCH = 4
U = 4


def steps(eng, head, full, hi, body):
    assert head % U == 0 and (full - head) % U == 0
    for i in range(head):
        body(i, i % U)
    with eng.Fori(0, (full - head) // U) as v:
        for k in range(U):
            body(v * U + (head + k), k)
    for i in range(full, hi):
        body(i, i % U)


def wait(eng, sem, n):
    if not (isinstance(n, int) and n <= 0):
        eng.wait_ge(sem, n)


def fixed_first(eng, sem, n, *later):
    for value in later:
        if not isinstance(value, int):
            eng.compute_val(value)
    eng.wait_ge(sem, n)


def stage(i, r, lag, count, fn):
    if isinstance(i, int) and not 0 <= i - lag < count:
        return
    fn(i - lag, (r - lag) % U)


def block_kernel(nc, x, Wq, bq, Wk, bk, Wv, bv, Wo, bo, m, Wr, W1, W2, out):
    ctx = ExitStack()
    with ctx:
        def sb(name, shape, dt=F32):
            return ctx.enter_context(nc.sbuf_tensor(name, shape, dt))

        def sem(name):
            return ctx.enter_context(nc.semaphore(name))

        x_sb = sb("x_sb", [P, NB, S * F])
        w1_sb = sb("w1_sb", [P, E, HID])
        w2_sb = sb("w2_sb", [P, E, HC * F])
        wqk = sb("wqk", [P, 2 * F])
        wvr = sb("wvr", [P, F + E])
        wo = sb("wo", [P, F])
        ident = sb("ident", [P, P])
        head_scale = sb("head_scale", [P, F])
        tri = sb("tri", [P, P], BF16)
        ones = sb("ones", [P, P], BF16)
        region0 = sb("region0", [1, S, E], BF16)
        NBIAS = 2 * F + F + E + F
        bias3 = sb("bias3", [3, NBIAS])
        rest3 = sb("rest3", [3, 2, NBIAS])
        part3 = sb("part3", [3, 2, NBIAS], BF16)
        pick3 = sb("pick3", [3, 3])
        sum3 = sb("sum3", [3, 2, NBIAS])
        bias_parts = sb("bias_parts", [3, NBIAS], BF16)
        out_bias2 = sb("out_bias2", [3, S, F], BF16)
        expert_no = sb("expert_no", [P, E])
        m_row = sb("m_row", [P, H])
        m_work = sb("m_work", [P, 4, H])
        rowi = sb("rowi", [P, 2], I32)
        coli = sb("coli", [P, 2, P], I32)
        rowf = sb("rowf", [P, 1])
        same_head = sb("same_head", [P, P])
        eps = sb("eps", [P, 1])
        rstd = sb("rstd", [P, TILES])
        shift = sb("shift", [P, TILES])
        info = sb("info", [P, TILES, 2])
        stats = sb("stats", [P, U, S, 6])
        meanvar = sb("meanvar", [P, U, S, 2])
        std = sb("std", [P, U, S])
        xn = sb("xn", [P, U, S * F])
        xnT = sb("xnT", [P, U, S * P])
        q_raw = sb("q_raw", [P, U, S * F])
        squares = sb("squares", [P, U, S * 2 * F])
        sumsq = sb("sumsq", [P, U, S * 2 * H])
        clamped = sb("clamped", [P, U, S * 2 * H])
        norm = sb("norm", [P, U, S * 2 * H])
        rnorm = sb("rnorm", [P, U, S, 2 * H])
        kn = sb("kn", [P, U, S * F])
        qn = sb("qn", [P, U, S * F])
        qnT = sb("qnT", [P, U, S * P])
        vr = sb("vr", [P, U, S, F + E])
        kvT = sb("kvT", [P, U, F])
        mat = sb("mat", [P, U, F])
        top8 = sb("top8", [P, U, S, E])
        topidx = sb("topidx", [P, U, S, E], U32)
        onehot = sb("onehot", [P, U, S, E], BF16)
        seen = sb("seen", [P, S, E], BF16)
        prefix1 = sb("prefix1", [P, U, S, E])
        place = sb("place", [P, U, S], I32)
        rows = sb("rows", [P, U, S, ROW])
        pad_rows = sb("pad_rows", [P, ROW])
        te = sb("te", [1, 6, E])
        te_i = sb("te_i", [1, 3, E], I32)
        tile_no = sb("tile_no", [1, FT])
        reached = sb("reached", [1, 2, FT, E])
        tj = sb("tj", [1, 3, FT])
        tile_expert = sb("tile_expert", [1, FT], I32)
        tile_row = sb("tile_row", [1, FT], I32)
        grows = sb("grows", [P, U, ROW])
        token = sb("token", [P, U, 1], I32)
        tanh_gap = sb("tanh_gap", [P, U, 1])
        weight = sb("weight", [P, U, 1])
        w1_now = sb("w1_now", [P, U, HID])
        gT = sb("gT", [P, U, P])
        hT = sb("hT", [P, U, HID])
        orows = sb("orows", [P, U, F])

        banks = [ctx.enter_context(nc.psum_tensor(f"bank{i}", [P, 512], F32)) for i in range(8)]
        turn_ps, vr_ps, kvT_ps, mat_ps, place_ps, o_ps = banks[0:6]
        qk_ps = banks[6:8]
        gT_ps, h_ps, y_ps = banks[0:2], banks[2:4], banks[4:6]

        rows_dram = nc.dram_tensor("rows_dram", (E * REGION + P, ROW), F32, kind="Internal").ap()

        x_loaded = [sem(f"x_loaded{c}") for c in range(NB // XCH)]
        w_loaded, bias_loaded, ffn_loaded = sem("w_loaded"), sem("bias_loaded"), sem("ffn_loaded")
        consts_pool, pool_chain = sem("consts_pool"), sem("pool_chain")
        dve_chain = sem("dve_chain")
        exp_m, sigmoid_m = sem("exp_m"), sem("sigmoid_m")
        bias_ready, scale_ready = sem("bias_ready"), sem("scale_ready")
        stats_ready, meanvar_ready, std_ready = sem("stats_ready"), sem("meanvar_ready"), sem("std_ready")
        rstd_ready, shift_ready = sem("rstd_ready"), sem("shift_ready")
        xn_ready = sem("xn_ready")
        xT_in_psum, xT_ready = sem("xT_in_psum"), sem("xT_ready")
        qk_in_psum, vr_in_psum = sem("qk_in_psum"), sem("vr_in_psum")
        q_ready, squares_ready, vr_ready = sem("q_ready"), sem("squares_ready"), sem("vr_ready")
        sumsq_ready, clamped_ready = sem("sumsq_ready"), sem("clamped_ready")
        norm_ready, rnorm_ready = sem("norm_ready"), sem("rnorm_ready")
        kn_ready, qn_ready = sem("kn_ready"), sem("qn_ready")
        qT_in_psum, qT_ready = sem("qT_in_psum"), sem("qT_ready")
        kvT_in_psum, kvT_ready = sem("kvT_in_psum"), sem("kvT_ready")
        mat_in_psum, mat_ready = sem("mat_in_psum"), sem("mat_ready")
        o_in_psum, sum_ready = sem("o_in_psum"), sem("sum_ready")
        top_ready, topidx_ready, gap_ready = sem("top_ready"), sem("topidx_ready"), sem("gap_ready")
        onehot_ready, seen_ready = sem("onehot_ready"), sem("seen_ready")
        prefix_in_psum, prefix1_ready, place_ready = sem("prefix_in_psum"), sem("prefix1_ready"), sem("place_ready")
        info_ready, rown_ready = sem("info_ready"), sem("rown_ready")
        scattered = [sem(f"scattered{r}") for r in range(U)]
        ends_in_psum, ends_ready, table_ready = sem("ends_in_psum"), sem("ends_ready"), sem("table_ready")
        pads_written = sem("pads_written")
        g_loaded = [sem(f"g_loaded{r}") for r in range(U)]
        token_ready, tanh_ready, weight_ready = sem("token_ready"), sem("tanh_ready"), sem("weight_ready")
        w1_staged = sem("w1_staged")
        gT_in_psum, gT_ready = sem("gT_in_psum"), sem("gT_ready")
        h_in_psum, hT_ready = sem("h_in_psum"), sem("hT_ready")
        y_in_psum, orows_ready = sem("y_in_psum"), sem("orows_ready")
        stored = [sem(f"stored{r}") for r in range(U)]

        x_dram = x.rearrange("b (p s) f -> p b (s f)", s=S)
        out_rows = out.rearrange("b t f -> (b t) f")

        def heads(ap):
            return ap.rearrange("p (g d) -> p g d", d=HD)

        def one(ap):
            return ap.rearrange("p a f -> p (a f)")

        def after_round(eng, sems, c, r, per_use):
            if not (isinstance(c, int) and c < U):
                eng.wait_ge(sems[r], (c - r) // U * per_use)

        HEAD1, END1 = 12, NB + 10
        HEAD2, END2 = 8, FT + 3
        ctx.enter_context(nc.allow_low_precision(reason="row numbers are integers below 2^24"))
        block = ctx.enter_context(nc.Block())

        @block.sync
        def _(sp):
            for c in range(NB // XCH):
                b = slice(c * XCH, (c + 1) * XCH)
                sp.dma_start(x_sb[:, b, :], x_dram[:, b, :]).then_inc(x_loaded[c], 16)
            sp.dma_start(w1_sb[:], W1.rearrange("e d h -> d e h")).then_inc(ffn_loaded, 16)
            sp.dma_start(w2_sb[:].rearrange("p e (c d) -> p e c d", c=HC),
                         W2.rearrange("e (c p) d -> p e c d", p=P)).then_inc(ffn_loaded, 16)
            sp.wait_ge(consts_pool, 1)
            sp.dma_start(rows_dram[E * REGION:E * REGION + P, :], pad_rows[:]).then_inc(pads_written, 16)
            sp.wait_ge(ends_ready, 1)
            for e in range(E):
                end = sp.value_load(te_i[0:1, 2, e:e + 1], min_val=0, max_val=E * REGION)
                sp.dma_start(rows_dram[bass.ds(end, P), :], pad_rows[:]).then_inc(pads_written, 16)

            sp.wait_ge(table_ready, 1)
            for r in range(U):
                sp.wait_ge(scattered[r], 16 * S * (NB // U))
            sp.wait_ge(pads_written, 16 * (E + 1))

            def load_rows(j, r):
                wait(sp, orows_ready, j - U + 1)
                wait(sp, token_ready, j - U + 1)
                wait(sp, gT_in_psum, j - U + 1)
                row = sp.value_load(tile_row[0:1, bass.ds(j, 1)], min_val=0, max_val=E * REGION)
                sp.dma_start(grows[:, r, :], rows_dram[bass.ds(row, P), :]).then_inc(g_loaded[r], 16)

            steps(sp, HEAD2, FT, FT, load_rows)
            for r in range(U):
                sp.wait_ge(stored[r], 16 * (FT // U))

        @block.gpsimd
        def _(pool):
            G = nc.gpsimd
            G.memset(pad_rows[:], 0.0).then_inc(pool_chain, 1)
            G.memset(ident[:], 0.0)
            G.memset(tri[:], 1.0)
            G.memset(ones[:], 1.0)
            G.memset(seen[:], 0.0)
            G.memset(eps[:], 1e-5)
            G.memset(pick3[:], 0.0).then_inc(pool_chain, 1)
            pool.wait_ge(pool_chain, 1)
            G.memset(pad_rows[:, TOK:TOK + 1], PAD_TOKEN).then_inc(consts_pool, 1)

            def iota(dst, pattern, lane):
                return G.iota(dst, pattern, base=0, channel_multiplier=lane, allow_small_or_imprecise_dtypes=True)

            iota(region0[0:1], [[0, S], [REGION, E]], 0)
            iota(expert_no[:], [[1, E]], 0)
            iota(tile_no[0:1, :], [[1, FT]], 0)
            iota(info[:, :, 0], [[NT, NB], [1, S]], S)
            iota(rowi[:, 0:1], [[0, 1]], 1)
            iota(coli[:, 0, :], [[1, P]], 0).then_inc(consts_pool, 1)
            pool.wait_ge(pool_chain, 2)
            G.affine_select(out=ident[:], in_=ident[:], compare_op=ALU.not_equal, fill=1.0, base=0,
                            pattern=[[-1, P]], channel_multiplier=1)
            G.affine_select(out=tri[:], in_=tri[:], compare_op=ALU.is_gt, fill=0.0, base=0,
                            pattern=[[1, P]], channel_multiplier=-1)
            G.affine_select(out=pick3[:], in_=pick3[:], compare_op=ALU.not_equal, fill=1.0, base=0,
                            pattern=[[-1, 3]], channel_multiplier=1).then_inc(consts_pool, 1)
            pool.wait_ge(consts_pool, 3)

            def clamp(c, r):
                fixed_first(pool, consts_pool, 3, c + 1, c - U + 1)
                pool.wait_ge(sumsq_ready, c + 1)
                wait(pool, norm_ready, c - U + 1)
                G.tensor_scalar(clamped[:, r, :], sumsq[:, r, :], 1e-24, None, ALU.max).then_inc(clamped_ready, 1)

            def scale_q(c, r):
                pool.wait_ge(rnorm_ready, c + 1)
                pool.wait_ge(q_ready, c + 1)
                wait(pool, qT_in_psum, c - U + 1)
                G.tensor_tensor(qn[:, r, :].rearrange("p (s g d) -> p s g d", s=S, d=HD),
                                q_raw[:, r, :].rearrange("p (s g d) -> p s g d", s=S, d=HD),
                                rnorm[:, r, :, 0:H].unsqueeze(3).broadcast_to([P, S, H, HD]),
                                ALU.mult).then_inc(qn_ready, 1)

            def logit_gap(c, r):
                pool.wait_ge(top_ready, c + 1)
                G.tensor_tensor(info[:, bass.ds(c * S, S), 1], top8[:, r, :, 0], top8[:, r, :, 1],
                                ALU.subtract).then_inc(gap_ready, 1)

            def copy_info(c, r):
                pool.wait_ge(gap_ready, c + 1)
                after_round(pool, scattered, c, r, 16 * S)
                G.tensor_copy(rows[:, r, :, TOK:ROW], info[:, bass.ds(c * S, S), :]).then_inc(info_ready, 1)

            def scatter(c, r):
                fixed_first(pool, consts_pool, 3, c + 1)
                pool.wait_ge(rown_ready, c + 1)
                pool.wait_ge(sum_ready, c + 1)
                pool.wait_ge(place_ready, c + 1)
                pool.wait_ge(info_ready, c + 1)
                for s in range(S):
                    G.indirect_dma_start(
                        rows_dram, bass.IndirectOffsetOnAxis(ap=place[:, r, s:s + 1], axis=0),
                        rows[:, r, s, :], None).then_inc(scattered[r], 16)

            def step1(i, r):
                stage(i, r, 10, NB, scatter)
                stage(i, r, 8, NB, copy_info)
                stage(i, r, 6, NB, logit_gap)
                stage(i, r, 5, NB, clamp)
                stage(i, r, 6, NB, scale_q)

            steps(pool, HEAD1, NB, END1, step1)

            def store(j, r):
                fixed_first(pool, table_ready, 1, j + 1)
                pool.wait_ge(orows_ready, j + 1)
                pool.wait_ge(token_ready, j + 1)
                G.indirect_dma_start(
                    out_rows, bass.IndirectOffsetOnAxis(ap=token[:, r, :], axis=0),
                    orows[:, r, :], None, bounds_check=TOKENS - 1, oob_is_err=False).then_inc(stored[r], 16)

            def step2(i, r):
                stage(i, r, 3, FT, store)

            steps(pool, HEAD2, FT, END2, step2)

        @block.scalar
        def _(act):
            A = nc.scalar
            act.dma_start(m_row[:], m.partition_broadcast(P)).then_inc(bias_loaded, 16)
            for n, b in enumerate((bq, bk, bv)):
                act.dma_start(bias3[:, n * F:(n + 1) * F], b.partition_broadcast(3)).then_inc(bias_loaded, 16)
            act.dma_start(bias3[:, NBIAS - F:NBIAS], bo.partition_broadcast(3)).then_inc(bias_loaded, 16)
            for dst, src in ((wqk[:, 0:F], Wq), (wqk[:, F:2 * F], Wk), (wvr[:, 0:F], Wv), (wvr[:, F:F + E], Wr),
                             (wo[:], Wo)):
                act.dma_start(dst, src).then_inc(w_loaded, 16)
            act.wait_ge(bias_loaded, 16 * 5)
            A.activation(m_work[:, 0, :], m_row[:], ACT.Exp, scale=-1.0).then_inc(exp_m, 1)
            act.wait_ge(sigmoid_m, 1)
            A.activation(m_work[:, 3, :], m_work[:, 2, :], ACT.Exp, scale=-float(np.log(NT))).then_inc(exp_m, 1)
            act.wait_ge(consts_pool, 3)

            def std_of(c, r):
                act.wait_ge(meanvar_ready, c + 1)
                wait(act, rstd_ready, c - U + 1)
                A.activation(std[:, r, :], meanvar[:, r, :, 1], ACT.Sqrt, bias=eps[:, 0:1]).then_inc(std_ready, 1)

            def normalised(dst, c, s):
                t = bass.ds(c * S + s, 1)
                return A.activation(dst, one(x_sb[:, bass.ds(c, 1), s * F:(s + 1) * F]), ACT.Identity,
                                    bias=shift[:, t], scale=rstd[:, t])

            def normalise(c, r):
                act.wait_ge(shift_ready, c + 1)
                wait(act, xT_in_psum, c - U + 1)
                for s in range(S):
                    ins = normalised(xn[:, r, s * F:(s + 1) * F], c, s)
                ins.then_inc(xn_ready, 1)

            def xT_copy(c, r):
                act.wait_ge(xT_in_psum, c + 1)
                wait(act, vr_in_psum, c - U + 1)
                A.copy(xnT[:, r, :], turn_ps[:, 0:S * P]).then_inc(xT_ready, 1)

            def take_qk(c, r):
                act.wait_ge(qk_in_psum, c + 1)
                wait(act, qn_ready, c - U + 1)
                A.copy(q_raw[:, r, :].rearrange("p (s f) -> p s f", s=S),
                       qk_ps[r % 2][:].rearrange("p (s f) -> p s f", s=S)[:, :, 0:F]).then_inc(q_ready, 1)
                wait(act, sumsq_ready, c - U + 1)
                A.activation(squares[:, r, :], qk_ps[r % 2][:], ACT.Square).then_inc(squares_ready, 1)

            def take_vr(c, r):
                act.wait_ge(vr_in_psum, c + 1)
                wait(act, kvT_in_psum, c - U + 1)
                wait(act, topidx_ready, c - U + 1)
                A.copy(vr[:, r], vr_ps[:, 0:S * (F + E)].rearrange("p (s f) -> p s f", s=S)).then_inc(vr_ready, 1)

            def norms(c, r):
                act.wait_ge(clamped_ready, c + 1)
                wait(act, rnorm_ready, c - U + 1)
                A.activation(norm[:, r, :], clamped[:, r, :], ACT.Sqrt).then_inc(norm_ready, 1)

            def qT_copy(c, r):
                act.wait_ge(qT_in_psum, c + 1)
                wait(act, o_in_psum, c - U + 1)
                A.copy(qnT[:, r, :], turn_ps[:, 0:S * P]).then_inc(qT_ready, 1)

            def mat_copy(c, r):
                act.wait_ge(mat_in_psum, c + 1)
                wait(act, o_in_psum, c - U + 1)
                A.copy(mat[:, r, :], mat_ps[:, 0:F]).then_inc(mat_ready, 1)

            def row_features(c, r):
                act.wait_ge(info_ready, c + 1)
                for s in range(S):
                    ins = normalised(rows[:, r, s, 0:F], c, s)
                ins.then_inc(rown_ready, 1)

            def step1(i, r):
                stage(i, r, 3, NB, xT_copy)
                stage(i, r, 1, NB, std_of)
                stage(i, r, 6, NB, norms)
                stage(i, r, 9, NB, row_features)
                stage(i, r, 7, NB, qT_copy)
                stage(i, r, 2, NB, normalise)
                stage(i, r, 8, NB, mat_copy)
                stage(i, r, 4, NB, take_qk)
                stage(i, r, 4, NB, take_vr)

            steps(act, HEAD1, NB, END1, step1)

            def tanh(j, r):
                act.wait_ge(g_loaded[r], (j - r) // U * 16 + 16)
                wait(act, weight_ready, j - U + 1)
                A.activation(tanh_gap[:, r, :], grows[:, r, GAP:GAP + 1], ACT.Tanh, scale=0.5).then_inc(tanh_ready, 1)

            def gelu(j, r):
                act.wait_ge(h_in_psum, j + 1)
                wait(act, y_in_psum, j - U + 1)
                A.activation(hT[:, r, :], h_ps[r % 2][:], ACT.Gelu).then_inc(hT_ready, 1)

            def step2(i, r):
                stage(i, r, 0, FT, tanh)
                stage(i, r, 1, FT, gelu)

            steps(act, HEAD2, FT, END2, step2)

        @block.vector
        def _(dve):
            V = nc.vector
            links = [0]

            def link(ins):
                links[0] += 1
                ins.then_inc(dve_chain, 1)
                dve.wait_ge(dve_chain, links[0])

            def split_biases():
                dve.wait_ge(bias_loaded, 16 * 5)
                link(V.memset(bias3[:, 3 * F:3 * F + E], 0.0))
                link(V.tensor_copy(part3[:, 0, :], bias3[:]))
                link(V.tensor_tensor(rest3[:, 0, :], bias3[:], part3[:, 0, :], ALU.subtract))
                link(V.tensor_copy(part3[:, 1, :], rest3[:, 0, :]))
                link(V.tensor_tensor(rest3[:, 1, :], rest3[:, 0, :], part3[:, 1, :], ALU.subtract))
                link(V.tensor_scalar(sum3[:, 0, :], part3[:, 0, :], pick3[:, 0:1], None, ALU.mult))
                link(V.scalar_tensor_tensor(out=sum3[:, 1, :], in0=part3[:, 1, :], scalar=pick3[:, 1:2],
                                            in1=sum3[:, 0, :], op0=ALU.mult, op1=ALU.add))
                link(V.scalar_tensor_tensor(out=bias_parts[:], in0=rest3[:, 1, :], scalar=pick3[:, 2:3],
                                            in1=sum3[:, 1, :], op0=ALU.mult, op1=ALU.add))
                V.tensor_copy(out_bias2[:], bias_parts[:, NBIAS - F:NBIAS].unsqueeze(1).broadcast_to([3, S, F])
                              ).then_inc(bias_ready, 1)

            def sigmoid_of_m():
                dve.wait_ge(exp_m, 1)
                link(V.tensor_scalar(m_work[:, 1, :], m_work[:, 0, :], 1.0, None, ALU.add))
                V.reciprocal(m_work[:, 2, :], m_work[:, 1, :]).then_inc(sigmoid_m, 1)

            def scale_matrix():
                link(V.tensor_scalar(rowi[:, 1:2], rowi[:, 0:1], 3, None, ALU.arith_shift_right))
                link(V.tensor_scalar(coli[:, 1, :], coli[:, 0, :], 3, None, ALU.arith_shift_right))
                link(V.tensor_copy(rowf[:], rowi[:, 1:2]))
                link(V.tensor_scalar(same_head[:], coli[:, 1, :], rowf[:, 0:1], None, ALU.is_equal))
                dve.wait_ge(exp_m, 2)
                V.tensor_tensor(heads(head_scale[:]), heads(same_head[:]),
                                m_work[:, 3, :].unsqueeze(2).broadcast_to([P, H, HD]), ALU.mult).then_inc(scale_ready, 1)

            def statistics(c, r):
                if isinstance(c, int):
                    dve.wait_ge(x_loaded[c // XCH], 16)
                if isinstance(c, int) and c == HEAD1 - 1:
                    for n in range(HEAD1 // XCH, NB // XCH):
                        dve.wait_ge(x_loaded[n], 16)
                wait(dve, meanvar_ready, c - U + 1)
                for s in range(S):
                    ins = V.bn_stats(stats[:, r, s, :], one(x_sb[:, bass.ds(c, 1), s * F:(s + 1) * F]))
                ins.then_inc(stats_ready, 1)

            def aggregate(c, r):
                fixed_first(dve, x_loaded[0], 16, c + 1, c - U + 1)
                dve.wait_ge(stats_ready, c + 1)
                wait(dve, shift_ready, c - U + 1)
                for s in range(S):
                    ins = V.bn_aggr(meanvar[:, r, s, :], stats[:, r, s, :])
                ins.then_inc(meanvar_ready, 1)

            def rstd_of(c, r):
                dve.wait_ge(std_ready, c + 1)
                V.reciprocal(rstd[:, bass.ds(c * S, S)], std[:, r, :]).then_inc(rstd_ready, 1)

            def shift_of(c, r):
                dve.wait_ge(rstd_ready, c + 1)
                V.scalar_tensor_tensor(out=shift[:, bass.ds(c * S, S)], in0=meanvar[:, r, :, 0], scalar=-1.0,
                                       in1=rstd[:, bass.ds(c * S, S)], op0=ALU.mult, op1=ALU.mult
                                       ).then_inc(shift_ready, 1)

            def sum_squares(c, r):
                dve.wait_ge(squares_ready, c + 1)
                wait(dve, clamped_ready, c - U + 1)
                V.tensor_reduce(sumsq[:, r, :], heads(squares[:, r, :]), AX.X, ALU.add).then_inc(sumsq_ready, 1)

            def top(c, r):
                fixed_first(dve, consts_pool, 3, c + 1, c - U + 1)
                dve.wait_ge(vr_ready, c + 1)
                wait(dve, gap_ready, c - U + 1)
                for s in range(S):
                    ins = V.max(top8[:, r, s, :], vr[:, r, s, F:F + E])
                ins.then_inc(top_ready, 1)

            def top_index(c, r):
                fixed_first(dve, consts_pool, 3, c + 1, c - U + 1)
                dve.wait_ge(top_ready, c + 1)
                wait(dve, onehot_ready, c - U + 1)
                for s in range(S):
                    ins = V.max_index(topidx[:, r, s, :], top8[:, r, s, :], vr[:, r, s, F:F + E])
                ins.then_inc(topidx_ready, 1)

            def one_hot(c, r):
                dve.wait_ge(topidx_ready, c + 1)
                wait(dve, seen_ready, c - U + 1)
                V.tensor_tensor(onehot[:, r], expert_no[:].unsqueeze(1).broadcast_to([P, S, E]),
                                topidx[:, r, :, 0:1].broadcast_to([P, S, E]), ALU.is_equal).then_inc(onehot_ready, 1)

            def mask_prefix(c, r):
                dve.wait_ge(prefix_in_psum, c + 1)
                wait(dve, place_ready, c - U + 1)
                V.tensor_tensor(prefix1[:, r], place_ps[:, 0:S * E].rearrange("p (s e) -> p s e", s=S),
                                onehot[:, r], ALU.mult).then_inc(prefix1_ready, 1)
                wait(dve, seen_ready, c)
                V.tensor_tensor(seen[:], seen[:], onehot[:, r], ALU.add).then_inc(seen_ready, 1)

            def find_place(c, r):
                dve.wait_ge(prefix1_ready, c + 1)
                after_round(dve, scattered, c, r, 16 * S)
                V.tensor_reduce(place[:, r, :], prefix1[:, r], AX.X, ALU.add).then_inc(place_ready, 1)

            def reciprocal_norms(c, r):
                dve.wait_ge(norm_ready, c + 1)
                wait(dve, qn_ready, c - U + 1)
                wait(dve, kn_ready, c - U + 1)
                V.reciprocal(rnorm[:, r].rearrange("p s h -> p (s h)"), norm[:, r, :]).then_inc(rnorm_ready, 1)

            def scale_k(c, r):
                dve.wait_ge(rnorm_ready, c + 1)
                dve.wait_ge(squares_ready, c + 1)
                wait(dve, kvT_in_psum, c - U + 1)
                V.tensor_tensor(kn[:, r, :].rearrange("p (s g d) -> p s g d", s=S, d=HD),
                                qk_ps[r % 2][:].rearrange("p (s g d) -> p s g d", s=S, d=HD)[:, :, H:2 * H, :],
                                rnorm[:, r, :, H:2 * H].unsqueeze(3).broadcast_to([P, S, H, HD]),
                                ALU.mult).then_inc(kn_ready, 1)

            def mask_kvT(c, r):
                dve.wait_ge(kvT_in_psum, c + 1)
                wait(dve, mat_in_psum, c - U + 1)
                V.tensor_tensor(kvT[:, r, :], kvT_ps[:, 0:F], head_scale[:], ALU.mult).then_inc(kvT_ready, 1)

            def add_attention(c, r):
                dve.wait_ge(o_in_psum, c + 1)
                dve.wait_ge(info_ready, c + 1)
                V.tensor_tensor(rows[:, r, :, F:2 * F], o_ps[:, 0:S * F].rearrange("p (s f) -> p s f", s=S),
                                one(x_sb[:, bass.ds(c, 1), :]).rearrange("p (s f) -> p s f", s=S), ALU.add
                                ).then_inc(sum_ready, 1)

            def list_ends():
                dve.wait_ge(ends_in_psum, 1)
                link(V.tensor_copy(te[0:1, 0, :], place_ps[0:1, 0:E]))
                V.tensor_copy(te_i[0:1, 2, :], te[0:1, 0, :]).then_inc(ends_ready, 1)
                link(V.tensor_tensor(te[0:1, 1, :], te[0:1, 0, :], region0[0:1, 0, :], ALU.subtract))
                link(V.tensor_scalar(te_i[0:1, 0, :], te[0:1, 1, :], float(P - 1), None, ALU.add))
                link(V.tensor_scalar(te_i[0:1, 1, :], te_i[0:1, 0, :], P.bit_length() - 1, None, ALU.arith_shift_right))
                link(V.tensor_copy(te[0:1, 2, :], te_i[0:1, 1, :]))
                link(V.memset(te[0:1, 3, :], 1.0))
                link(V.tensor_tensor_scan(te[0:1, 4, :], te[0:1, 3, :], te[0:1, 2, :], 0.0, ALU.mult, ALU.add))
                link(V.tensor_scalar(te[0:1, 5, :], te[0:1, 2, :], -float(P), float(REGION), ALU.mult, ALU.add))
                link(V.tensor_tensor(reached[0:1, 0], tile_no[0:1, :].unsqueeze(2).broadcast_to([1, FT, E]),
                                     te[0:1, 4, :].unsqueeze(1).broadcast_to([1, FT, E]), ALU.is_ge))
                link(V.tensor_reduce(tj[0:1, 0, :], reached[0:1, 0], AX.X, ALU.add))
                link(V.tensor_tensor(reached[0:1, 1], reached[0:1, 0],
                                     te[0:1, 5, :].unsqueeze(1).broadcast_to([1, FT, E]), ALU.mult))
                link(V.tensor_reduce(tj[0:1, 1, :], reached[0:1, 1], AX.X, ALU.add))
                link(V.scalar_tensor_tensor(out=tj[0:1, 2, :], in0=tile_no[0:1, :], scalar=float(P),
                                            in1=tj[0:1, 1, :], op0=ALU.mult, op1=ALU.add))
                link(V.tensor_scalar(tile_expert[0:1, :], tj[0:1, 0, :], float(E - 1), None, ALU.min))
                V.tensor_scalar(tile_row[0:1, :], tj[0:1, 2, :], float(E * REGION), None, ALU.min
                                ).then_inc(table_ready, 1)

            def step1(i, r):
                if isinstance(i, int) and i == 1:
                    dve.wait_ge(consts_pool, 3)
                    sigmoid_of_m()
                if isinstance(i, int) and i == 3:
                    split_biases()
                if isinstance(i, int) and i == 4:
                    scale_matrix()
                stage(i, r, 6, NB, reciprocal_norms)
                stage(i, r, 7, NB, mask_prefix)
                stage(i, r, 1, NB, rstd_of)
                stage(i, r, 6, NB, scale_k)
                stage(i, r, 7, NB, find_place)
                stage(i, r, 1, NB, shift_of)
                stage(i, r, 5, NB, top)
                stage(i, r, 7, NB, mask_kvT)
                stage(i, r, 5, NB, top_index)
                stage(i, r, 0, NB, statistics)
                stage(i, r, 5, NB, one_hot)
                stage(i, r, 5, NB, sum_squares)
                stage(i, r, 0, NB, aggregate)
                stage(i, r, 9, NB, add_attention)
                if isinstance(i, int) and i == NB + 7:
                    list_ends()

            steps(dve, HEAD1, NB, END1, step1)

            dve.wait_ge(ffn_loaded, 32)

            def stage_w1(j, r):
                e = dve.value_load(tile_expert[0:1, bass.ds(j, 1)], min_val=0, max_val=E - 1)
                wait(dve, h_in_psum, j - U + 1)
                V.tensor_copy(w1_now[:, r, :], one(w1_sb[:, bass.ds(e, 1), :])).then_inc(w1_staged, 1)

            def gT_copy(j, r):
                dve.wait_ge(gT_in_psum, j + 1)
                wait(dve, h_in_psum, j - U + 1)
                V.tensor_copy(gT[:, r, :], gT_ps[r % 2][:, 0:P]).then_inc(gT_ready, 1)

            def token_of(j, r):
                dve.wait_ge(g_loaded[r], (j - r) // U * 16 + 16)
                after_round(dve, stored, j, r, 16)
                V.tensor_copy(token[:, r, :], grows[:, r, TOK:TOK + 1]).then_inc(token_ready, 1)

            def weight_of(j, r):
                dve.wait_ge(tanh_ready, j + 1)
                wait(dve, orows_ready, j - U + 1)
                V.tensor_scalar(weight[:, r, :], tanh_gap[:, r, :], 0.5, 0.5, ALU.mult, ALU.add
                                ).then_inc(weight_ready, 1)

            def finish(j, r):
                dve.wait_ge(y_in_psum, j + 1)
                dve.wait_ge(weight_ready, j + 1)
                after_round(dve, stored, j, r, 16)
                V.scalar_tensor_tensor(out=orows[:, r, :], in0=y_ps[r % 2][:, 0:F], scalar=weight[:, r, :],
                                       in1=grows[:, r, F:2 * F], op0=ALU.mult, op1=ALU.add
                                       ).then_inc(orows_ready, 1)

            def step2(i, r):
                stage(i, r, 0, FT, gT_copy)
                stage(i, r, 0, FT, stage_w1)
                stage(i, r, 1, FT, weight_of)
                stage(i, r, 2, FT, finish)
                stage(i, r, 0, FT, token_of)

            steps(dve, HEAD2, FT, END2, step2)

        @block.tensor
        def _(pe):
            T = nc.tensor
            pe.wait_ge(w_loaded, 16 * 5)
            pe.wait_ge(consts_pool, 3)

            def transposes(c, r):
                pe.wait_ge(xn_ready, c + 1)
                wait(pe, qT_ready, c - 4)
                for s in range(S):
                    ins = T.transpose(turn_ps[:, s * P:(s + 1) * P], xn[:, r, s * F:(s + 1) * F], ident[:])
                ins.then_inc(xT_in_psum, 1)

            def q_transposes(c, r):
                pe.wait_ge(qn_ready, c + 1)
                pe.wait_ge(xT_ready, c + 5 if not isinstance(c, int) else min(c + 5, NB))
                for s in range(S):
                    ins = T.transpose(turn_ps[:, s * P:(s + 1) * P], qn[:, r, s * F:(s + 1) * F], ident[:])
                ins.then_inc(qT_in_psum, 1)

            def project(c, r):
                if isinstance(c, int) and c == 0:
                    pe.wait_ge(bias_ready, 1)
                pe.wait_ge(xT_ready, c + 1)
                wait(pe, vr_ready, c)
                for s in range(S):
                    o = vr_ps[:, s * (F + E):(s + 1) * (F + E)]
                    T.matmul(o, ones[0:3, :], bias_parts[:, 2 * F:3 * F + E], start=True, stop=False)
                    ins = T.matmul(o, xnT[:, r, s * P:(s + 1) * P], wvr[:], start=False, stop=True)
                ins.then_inc(vr_in_psum, 1)
                wait(pe, kn_ready, c - 1)
                for s in range(S):
                    o = qk_ps[r % 2][:, s * 2 * F:(s + 1) * 2 * F]
                    T.matmul(o, ones[0:3, :], bias_parts[:, 0:2 * F], start=True, stop=False)
                    ins = T.matmul(o, xnT[:, r, s * P:(s + 1) * P], wqk[:], start=False, stop=True)
                ins.then_inc(qk_in_psum, 1)

            def earlier_tokens(last):
                T.matmul(place_ps[:, 0:S * E], ones[0:1, :], region0[0:1], start=True, stop=False)
                for s in range(S):
                    ins = T.matmul(place_ps[:, 0:S * E], ones[:], seen[:, s:s + 1, :].broadcast_to([P, S, E]),
                                   start=False, stop=last and s == S - 1)
                return ins

            def prefixes(c, r):
                pe.wait_ge(onehot_ready, c + 1)
                wait(pe, seen_ready, c)
                wait(pe, prefix1_ready, c)
                earlier_tokens(False)
                T.matmul(place_ps[:, E:2 * E], ones[:], onehot[:, r, 0, :], start=False, stop=False)
                T.matmul(place_ps[:, 0:S * E], tri[:], onehot[:, r], start=False, stop=True
                         ).then_inc(prefix_in_psum, 1)

            def kv_product(c, r):
                pe.wait_ge(kn_ready, c + 1)
                pe.wait_ge(vr_ready, c + 1)
                wait(pe, kvT_ready, c)
                for s in range(S):
                    ins = T.matmul(kvT_ps[:, 0:F], vr[:, r, s, 0:F], kn[:, r, s * F:(s + 1) * F],
                                   start=(s == 0), stop=(s == S - 1))
                ins.then_inc(kvT_in_psum, 1)

            def with_wo(c, r):
                pe.wait_ge(kvT_ready, c + 1)
                wait(pe, mat_ready, c)
                T.matmul(mat_ps[:, 0:F], kvT[:, r, :], wo[:], start=True, stop=True).then_inc(mat_in_psum, 1)

            def attend(c, r):
                pe.wait_ge(qT_ready, c + 1)
                pe.wait_ge(mat_ready, c + 1)
                wait(pe, sum_ready, c)
                T.matmul(o_ps[:, 0:S * F], ones[0:3, :], out_bias2[:].rearrange("p s f -> p (s f)"),
                         start=True, stop=False)
                for s in range(S):
                    ins = T.matmul(o_ps[:, s * F:(s + 1) * F], qnT[:, r, s * P:(s + 1) * P], mat[:, r, :],
                                   start=False, stop=(s == S - 1))
                ins.then_inc(o_in_psum, 1)

            def step1(i, r):
                stage(i, r, 3, NB, transposes)
                stage(i, r, 7, NB, prefixes)
                stage(i, r, 7, NB, kv_product)
                stage(i, r, 9, NB, attend)
                stage(i, r, 7, NB, q_transposes)
                stage(i, r, 8, NB, with_wo)
                stage(i, r, 4, NB, project)
                if isinstance(i, int) and i == NB + 7:
                    pe.wait_ge(seen_ready, NB)
                    pe.wait_ge(prefix1_ready, NB)
                    earlier_tokens(True).then_inc(ends_in_psum, 1)

            steps(pe, HEAD1, NB, END1, step1)

            pe.wait_ge(table_ready, 1)
            pe.wait_ge(ffn_loaded, 32)
            pe.wait_ge(qT_ready, NB)
            pe.wait_ge(kvT_ready, NB)
            pe.wait_ge(mat_ready, NB)
            pe.wait_ge(sum_ready, NB)

            def g_transpose(j, r):
                pe.wait_ge(g_loaded[r], (j - r) // U * 16 + 16)
                wait(pe, gT_ready, j - 1)
                T.transpose(gT_ps[r % 2][:, 0:P], grows[:, r, 0:F], ident[:]).then_inc(gT_in_psum, 1)

            def up(j, r):
                pe.wait_ge(gT_ready, j + 1)
                pe.wait_ge(w1_staged, j + 1)
                wait(pe, hT_ready, j - 1)
                for n in range(HC):
                    ins = T.matmul(h_ps[r % 2][:, n * P:(n + 1) * P], w1_now[:, r, n * P:(n + 1) * P],
                                   gT[:, r, :], start=True, stop=True)
                ins.then_inc(h_in_psum, 1)

            def down(j, r):
                e = pe.value_load(tile_expert[0:1, bass.ds(j, 1)], min_val=0, max_val=E - 1)
                pe.wait_ge(hT_ready, j + 1)
                wait(pe, orows_ready, j - 1)
                for n in range(HC):
                    ins = T.matmul(y_ps[r % 2][:, 0:F], hT[:, r, n * P:(n + 1) * P],
                                   one(w2_sb[:, bass.ds(e, 1), n * F:(n + 1) * F]),
                                   start=(n == 0), stop=(n == HC - 1))
                ins.then_inc(y_in_psum, 1)

            def step2(i, r):
                stage(i, r, 0, FT, g_transpose)
                stage(i, r, 1, FT, up)
                stage(i, r, 2, FT, down)

            steps(pe, HEAD2, FT, END2, step2)


_INS = ["L0_attn_x", "L0_attn_Wq", "L0_attn_bq", "L0_attn_Wk", "L0_attn_bk", "L0_attn_Wv", "L0_attn_bv",
        "L0_attn_Wo", "L0_attn_bo", "L0_attn_m", "L0_ffn_Wr", "L0_ffn_W1", "L0_ffn_W2"]
_OUTS = [((NB, NT, F), "float32")]


def kernel(**inputs):
    import numpy as _np
    import concourse.bacc as _bacc
    from concourse import mybir as _mybir
    from concourse.bass_utils import run_bass_kernel_spmd as _run

    nc = _bacc.Bacc("TRN2", target_bir_lowering=False, num_devices=1)
    arrays, args = {}, []
    for name in _INS:
        a = _np.ascontiguousarray(inputs[name])
        arrays[f"in_{name}_dram"] = a
        args.append(nc.dram_tensor(f"in_{name}_dram", a.shape, _mybir.dt.from_np(a.dtype), kind="ExternalInput").ap())
    for i, (shape, dtype) in enumerate(_OUTS):
        dt = _mybir.dt.from_np(_np.dtype(dtype))
        args.append(nc.dram_tensor(f"out_{i}_dram", shape, dt, kind="ExternalOutput").ap())
    block_kernel(nc, *args)
    r = _run(nc, [arrays], core_ids=[0])
    got = tuple(r.results[0][f"out_{i}_dram"] for i in range(len(_OUTS)))
    return got[0]
```

```python
from contextlib import ExitStack

import numpy as np
import concourse.bass as bass
from concourse import mybir

F32 = mybir.dt.float32
BF16 = mybir.dt.bfloat16
I32 = mybir.dt.int32
U32 = mybir.dt.uint32
ALU = mybir.AluOpType
ACT = mybir.ActivationFunctionType
AX = mybir.AxisListType

P = 128
NB, NT, F = 32, 256, 128
S = NT // P
TILES = NB * S
TOKENS = NB * NT
H, HD = 16, 8
E, HID = 8, 512
HC = HID // P
REGION = 8448
assert REGION >= TOKENS + P and REGION % 256 == 0
TOK, GAP = 2 * F, 2 * F + 1
ROW = 2 * F + 2
PAD_TOKEN = float(1 << 20)
FT = TOKENS // P + E - 1
WARM_UP = {4: 20, 5: 5, FT: 28}
X_LOADS = [range(b, b + 1) for b in range(4)] + [range(b, b + 4) for b in range(4, NB, 4)]
U, U2 = 4, 8


def steps(eng, u, head, full, hi, body):
    assert (full - head) % u == 0
    for i in range(head):
        body(i, i % u)
    with eng.Fori(0, (full - head) // u) as v:
        for k in range(u):
            body(v * u + (head + k), (head + k) % u)
    for i in range(full, hi):
        body(i, i % u)


def wait(eng, sem, n):
    if not (isinstance(n, int) and n <= 0):
        eng.wait_ge(sem, n)


def fixed_first(eng, sem, n, *later):
    for value in later:
        if not isinstance(value, int):
            eng.compute_val(value)
    eng.wait_ge(sem, n)


def stage(u, i, r, lag, count, fn):
    if isinstance(i, int) and not 0 <= i - lag < count:
        return
    fn(i - lag, (r - lag) % u)


def block_kernel(nc, x, Wq, bq, Wk, bk, Wv, bv, Wo, bo, m, Wr, W1, W2, out):
    ctx = ExitStack()
    with ctx:
        def sb(name, shape, dt=F32):
            return ctx.enter_context(nc.sbuf_tensor(name, shape, dt))

        def sem(name):
            return ctx.enter_context(nc.semaphore(name))

        x_sb = sb("x_sb", [P, NB, S * F])
        w1_sb = sb("w1_sb", [P, E, HID])
        w2_sb = sb("w2_sb", [P, E, HC * F])
        wqk = sb("wqk", [P, 2 * F])
        wvr = sb("wvr", [P, F + E])
        wo = sb("wo", [P, F])
        ident = sb("ident", [P, P])
        head_scale = sb("head_scale", [P, F])
        tri = sb("tri", [P, P], BF16)
        ones = sb("ones", [P, P], BF16)
        region0 = sb("region0", [1, S, E], BF16)
        NBIAS = 2 * F + F + E + F
        bias3 = sb("bias3", [3, NBIAS])
        rest3 = sb("rest3", [3, 2, NBIAS])
        part3 = sb("part3", [3, 2, NBIAS], BF16)
        below = sb("below", [3, 2])
        bias_parts = sb("bias_parts", [3, NBIAS], BF16)
        expert_no = sb("expert_no", [P, E])
        m_row = sb("m_row", [P, H])
        m_work = sb("m_work", [P, 4, H])
        rowi = sb("rowi", [P, 2], I32)
        coli = sb("coli", [P, 2, P], I32)
        rowf = sb("rowf", [P, 1])
        same_head = sb("same_head", [P, P])
        eps = sb("eps", [P, 1])
        tile_no = sb("tile_no", [P, 1])
        first_tile = sb("first_tile", [P, E])
        ones8 = sb("ones8", [P, E])
        rstd = sb("rstd", [P, TILES])
        shift = sb("shift", [P, TILES])
        info = sb("info", [P, TILES, 2])
        stats = sb("stats", [P, U, S, 6])
        meanvar = sb("meanvar", [P, U, S, 2])
        std = sb("std", [P, U * S])
        xn = sb("xn", [P, U, S * F])
        xnT = sb("xnT", [P, U, S * P])
        q_raw = sb("q_raw", [P, U, S * F])
        squares = sb("squares", [P, U, S * 2 * F])
        sumsq = sb("sumsq", [P, U, S * 2 * H])
        clamped = sb("clamped", [P, U, S * 2 * H])
        norm = sb("norm", [P, U, S * 2 * H])
        rnorm = sb("rnorm", [P, U, S, 2 * H])
        kn = sb("kn", [P, U, S * F])
        qn = sb("qn", [P, U, S * F])
        qnT = sb("qnT", [P, U, S * P])
        vr = sb("vr", [P, U, S, F + E])
        kvT = sb("kvT", [P, U, F])
        mat = sb("mat", [P, U, F])
        top8 = sb("top8", [P, U, S, E])
        topidx = sb("topidx", [P, U, S, E], U32)
        onehot = sb("onehot", [P, U, S, E], BF16)
        seen = sb("seen", [P, S, E], BF16)
        prefix1 = sb("prefix1", [P, U, S, E])
        place = sb("place", [P, U, S], I32)
        rows = sb("rows", [P, U, S, ROW])
        pad_rows = sb("pad_rows", [P, ROW])
        ends_i = sb("ends_i", [1, E], I32)
        up_i = sb("up_i", [P, 2, E], I32)
        tiles = sb("tiles", [P, 3, E])
        reached = sb("reached", [P, 2, E])
        entry = sb("entry", [P, 5])
        table = sb("table", [1, 2, P], I32)
        grows = sb("grows", [P, U2, ROW])
        token = sb("token", [P, U2, 1], I32)
        tanh_gap = sb("tanh_gap", [P, U2, 1])
        weight = sb("weight", [P, U2, 1])
        w1_now = sb("w1_now", [P, U2, HID])
        gT = sb("gT", [P, U2, P])
        hT = sb("hT", [P, U2, HID])
        orows = sb("orows", [P, U2, F])

        banks = [ctx.enter_context(nc.psum_tensor(f"bank{i}", [P, 512], F32)) for i in range(8)]
        turn_ps, vr_ps, kvT_ps, mat_ps, place_ps, o_ps = banks[0:6]
        qk_ps = banks[6:8]
        gT_ps, h_ps, y_ps = banks[0:2], banks[2:4], banks[4:6]

        rows_dram = nc.dram_tensor("rows_dram", (E * REGION + P, ROW), F32, kind="Internal").ap()

        x_loaded = [sem(f"x_loaded{n}") for n in range(len(X_LOADS))]
        m_loaded, w_loaded, bias_loaded, ffn_loaded = sem("m_loaded"), sem("w_loaded"), sem("bias_loaded"), sem("ffn_loaded")
        consts_pool, pool_chain = sem("consts_pool"), sem("pool_chain")
        dve_chain = sem("dve_chain")
        exp_m, sigmoid_m = sem("exp_m"), sem("sigmoid_m")
        bias_ready, scale_ready = sem("bias_ready"), sem("scale_ready")
        stats_ready, meanvar_ready, std_ready = sem("stats_ready"), sem("meanvar_ready"), sem("std_ready")
        rstd_ready, shift_ready = sem("rstd_ready"), sem("shift_ready")
        xn_ready = sem("xn_ready")
        xT_in_psum, xT_ready = sem("xT_in_psum"), sem("xT_ready")
        qk_in_psum, vr_in_psum = sem("qk_in_psum"), sem("vr_in_psum")
        q_ready, squares_ready, vr_ready = sem("q_ready"), sem("squares_ready"), sem("vr_ready")
        sumsq_ready, clamped_ready = sem("sumsq_ready"), sem("clamped_ready")
        norm_ready, rnorm_ready = sem("norm_ready"), sem("rnorm_ready")
        kn_ready, qn_ready = sem("kn_ready"), sem("qn_ready")
        qT_in_psum, qT_ready = sem("qT_in_psum"), sem("qT_ready")
        kvT_in_psum, kvT_ready = sem("kvT_in_psum"), sem("kvT_ready")
        mat_in_psum, mat_ready = sem("mat_in_psum"), sem("mat_ready")
        o_in_psum, sum_ready = sem("o_in_psum"), sem("sum_ready")
        top_ready, topidx_ready, gap_ready = sem("top_ready"), sem("topidx_ready"), sem("gap_ready")
        onehot_ready, seen_ready = sem("onehot_ready"), sem("seen_ready")
        prefix_in_psum, prefix1_ready, place_ready = sem("prefix_in_psum"), sem("prefix1_ready"), sem("place_ready")
        info_ready, rown_ready = sem("info_ready"), sem("rown_ready")
        scattered = [sem(f"scattered{r}") for r in range(U)]
        ends_in_psum, ends_ready = sem("ends_in_psum"), sem("ends_ready")
        entries_ready, table_in_psum, table_ready = sem("entries_ready"), sem("table_in_psum"), sem("table_ready")
        pads_written = sem("pads_written")
        g_loaded = [sem(f"g_loaded{r}") for r in range(U2)]
        token_ready, tanh_ready, weight_ready = sem("token_ready"), sem("tanh_ready"), sem("weight_ready")
        w1_staged = sem("w1_staged")
        gT_in_psum, gT_ready = sem("gT_in_psum"), sem("gT_ready")
        h_in_psum, hT_ready = sem("h_in_psum"), sem("hT_ready")
        y_in_psum, orows_ready = sem("y_in_psum"), sem("orows_ready")
        stored = [sem(f"stored{r}") for r in range(U2)]

        def write_pads(eng, experts):
            for e in experts:
                end = eng.value_load(ends_i[0:1, e:e + 1], min_val=0, max_val=E * REGION)
                eng.dma_start(rows_dram[bass.ds(end, P), :], pad_rows[:]).then_inc(pads_written, 16)

        x_dram = x.rearrange("b (p s) f -> p b (s f)", s=S)
        out_rows = out.rearrange("b t f -> (b t) f")

        def heads(ap):
            return ap.rearrange("p (g d) -> p g d", d=HD)

        def one(ap):
            return ap.rearrange("p a f -> p (a f)")

        def after_round(eng, sems, c, r, per_use):
            u = len(sems)
            if not (isinstance(c, int) and c < u):
                eng.wait_ge(sems[r], (c - r) // u * per_use)

        HEAD1, END1 = 12, NB + 10
        HEAD2, END2 = 15, FT + 4
        ctx.enter_context(nc.allow_low_precision(reason="row numbers are integers below 2^24"))
        block = ctx.enter_context(nc.Block())

        @block.sync
        def _(sp):
            def load_x(n):
                b = slice(X_LOADS[n].start, X_LOADS[n].stop)
                sp.dma_start(x_sb[:, b, :], x_dram[:, b, :]).then_inc(x_loaded[n], 16)

            for n in range(4):
                load_x(n)
            for n, b in enumerate((bq, bk, bv)):
                sp.dma_start(bias3[:, n * F:(n + 1) * F], b.partition_broadcast(3)).then_inc(bias_loaded, 16)
            sp.dma_start(bias3[:, NBIAS - F:NBIAS], bo.partition_broadcast(3)).then_inc(bias_loaded, 16)
            for dst, src in ((wvr[:, 0:F], Wv), (wvr[:, F:F + E], Wr), (wqk[:, 0:F], Wq), (wqk[:, F:2 * F], Wk),
                             (wo[:], Wo)):
                sp.dma_start(dst, src).then_inc(w_loaded, 16)
            for n in range(4, len(X_LOADS)):
                load_x(n)
            sp.wait_ge(consts_pool, 1)
            sp.dma_start(rows_dram[E * REGION:E * REGION + P, :], pad_rows[:]).then_inc(pads_written, 16)
            for e in range(E):
                sp.wait_ge(place_ready, 2 * e + 1)
                sp.dma_start(w1_sb[:, e, :], W1[e]).then_inc(ffn_loaded, 16)
                sp.dma_start(w2_sb[:, e, :].rearrange("p (c d) -> p c d", c=HC),
                             W2[e].rearrange("(c p) d -> p c d", p=P)).then_inc(ffn_loaded, 16)
            sp.wait_ge(ends_ready, 1)
            write_pads(sp, range(E // 2))

            sp.wait_ge(table_ready, 1)
            for r in range(U):
                sp.wait_ge(scattered[r], 16 * S * (NB // U))
            sp.wait_ge(pads_written, 16 * (E + 1))

            def load_rows(j, r):
                wait(sp, orows_ready, j - U2 + 1)
                wait(sp, token_ready, j - U2 + 1)
                wait(sp, gT_in_psum, j - U2 + 1)
                row = sp.value_load(table[0:1, 1, bass.ds(j, 1)], min_val=0, max_val=E * REGION)
                sp.dma_start(grows[:, r, :], rows_dram[bass.ds(row, P), :]).then_inc(g_loaded[r], 16)

            steps(sp, U2, HEAD2, FT, FT, load_rows)
            for r in range(U2):
                sp.wait_ge(stored[r], 16 * len(range(r, FT, U2)))

        @block.gpsimd
        def _(pool):
            G = nc.gpsimd
            G.memset(pad_rows[:], 0.0).then_inc(pool_chain, 1)
            G.memset(ident[:], 0.0)
            G.memset(tri[:], 1.0)
            G.memset(ones[:], 1.0)
            G.memset(seen[:], 0.0)
            G.memset(eps[:], 1e-5)
            G.memset(ones8[:], 1.0)
            G.memset(below[:], -1.0).then_inc(pool_chain, 1)
            pool.wait_ge(pool_chain, 1)
            G.memset(pad_rows[:, TOK:TOK + 1], PAD_TOKEN).then_inc(consts_pool, 1)

            def iota(dst, pattern, lane):
                return G.iota(dst, pattern, base=0, channel_multiplier=lane, allow_small_or_imprecise_dtypes=True)

            iota(region0[0:1], [[0, S], [REGION, E]], 0)
            iota(expert_no[:], [[1, E]], 0)
            iota(tile_no[:], [[0, 1]], 1)
            iota(first_tile[:], [[REGION // P, E]], 0)
            iota(info[:, :, 0], [[NT, NB], [1, S]], S)
            iota(rowi[:, 0:1], [[0, 1]], 1)
            iota(coli[:, 0, :], [[1, P]], 0).then_inc(consts_pool, 1)
            pool.wait_ge(pool_chain, 2)
            G.affine_select(out=ident[:], in_=ident[:], compare_op=ALU.not_equal, fill=1.0, base=0,
                            pattern=[[-1, P]], channel_multiplier=1)
            G.affine_select(out=tri[:], in_=tri[:], compare_op=ALU.is_gt, fill=0.0, base=0,
                            pattern=[[1, P]], channel_multiplier=-1)
            G.affine_select(out=below[:], in_=below[:], compare_op=ALU.is_gt, fill=0.0, base=0,
                            pattern=[[-1, 2]], channel_multiplier=1).then_inc(consts_pool, 1)
            pool.wait_ge(consts_pool, 3)

            def scale_q(c, r):
                pool.wait_ge(rnorm_ready, c + 1)
                pool.wait_ge(q_ready, c + 1)
                wait(pool, qT_in_psum, c - U + 1)
                G.tensor_tensor(qn[:, r, :].rearrange("p (s g d) -> p s g d", s=S, d=HD),
                                q_raw[:, r, :].rearrange("p (s g d) -> p s g d", s=S, d=HD),
                                rnorm[:, r, :, 0:H].unsqueeze(3).broadcast_to([P, S, H, HD]),
                                ALU.mult).then_inc(qn_ready, 1)

            def logit_gap(c, r):
                pool.wait_ge(top_ready, c + 1)
                G.tensor_tensor(info[:, bass.ds(c * S, S), 1], top8[:, r, :, 0], top8[:, r, :, 1],
                                ALU.subtract).then_inc(gap_ready, 1)

            def copy_info(c, r):
                pool.wait_ge(gap_ready, c + 1)
                after_round(pool, scattered, c, r, 16 * S)
                G.tensor_copy(rows[:, r, :, TOK:ROW], info[:, bass.ds(c * S, S), :]).then_inc(info_ready, 1)

            def scatter(c, r):
                fixed_first(pool, consts_pool, 3, c + 1)
                pool.wait_ge(rown_ready, c + 1)
                pool.wait_ge(sum_ready, c + 1)
                pool.wait_ge(place_ready, c + 1)
                pool.wait_ge(info_ready, c + 1)
                for s in range(S):
                    G.indirect_dma_start(
                        rows_dram, bass.IndirectOffsetOnAxis(ap=place[:, r, s:s + 1], axis=0),
                        rows[:, r, s, :], None).then_inc(scattered[r], 16)

            def step1(i, r):
                stage(U, i, r, 8, NB, scale_q)
                stage(U, i, r, 8, NB, copy_info)
                stage(U, i, r, 10, NB, scatter)
                stage(U, i, r, 7, NB, logit_gap)

            steps(pool, U, HEAD1, NB, END1, step1)

            def store(j, r):
                fixed_first(pool, table_ready, 1, j + 1)
                pool.wait_ge(orows_ready, j + 1)
                pool.wait_ge(token_ready, j + 1)
                G.indirect_dma_start(
                    out_rows, bass.IndirectOffsetOnAxis(ap=token[:, r, :], axis=0),
                    orows[:, r, :], None, bounds_check=TOKENS - 1, oob_is_err=False).then_inc(stored[r], 16)

            def step2(i, r):
                stage(U2, i, r, 4, FT, store)

            steps(pool, U2, HEAD2, FT, END2, step2)

        @block.scalar
        def _(act):
            A = nc.scalar
            act.dma_start(m_row[:], m.partition_broadcast(P)).then_inc(m_loaded, 16)
            act.wait_ge(m_loaded, 16)
            A.activation(m_work[:, 0, :], m_row[:], ACT.Exp, scale=-1.0).then_inc(exp_m, 1)
            act.wait_ge(sigmoid_m, 1)
            A.activation(m_work[:, 3, :], m_work[:, 2, :], ACT.Exp, scale=-float(np.log(NT))).then_inc(exp_m, 1)
            act.wait_ge(consts_pool, 3)
            A.activation(m_work[:, 0, 0:1], eps[:], ACT.Sqrt)

            def std_of(c, r):
                if r != U - 1:
                    return
                act.wait_ge(meanvar_ready, c + 1)
                wait(act, rstd_ready, (c - r) // U)
                A.activation(std[:], meanvar[:].rearrange("p u s t -> p (u s) t")[:, :, 1], ACT.Sqrt,
                             bias=eps[:, 0:1]).then_inc(std_ready, 1)

            def normalised(dst, c, s):
                t = bass.ds(c * S + s, 1)
                return A.activation(dst, one(x_sb[:, bass.ds(c, 1), s * F:(s + 1) * F]), ACT.Identity,
                                    bias=shift[:, t], scale=rstd[:, t])

            def normalise(s):
                def of_batch(c, r):
                    act.wait_ge(shift_ready, (c - r) // U + 1)
                    wait(act, xT_in_psum, c - U + 1)
                    wait(act, rown_ready, c - U + 1)
                    normalised(xn[:, r, s * F:(s + 1) * F], c, s).then_inc(xn_ready, 1)
                return of_batch

            def xT_copy(c, r):
                act.wait_ge(xT_in_psum, c + 1)
                wait(act, vr_in_psum, c - U + 1)
                A.copy(xnT[:, r, :], turn_ps[:, 0:S * P]).then_inc(xT_ready, 1)

            def take_qk(c, r):
                act.wait_ge(qk_in_psum, c + 1)
                wait(act, qn_ready, c - U + 1)
                wait(act, sumsq_ready, c - U + 1)
                A.activation(squares[:, r, :], qk_ps[r % 2][:], ACT.Square).then_inc(squares_ready, 1)
                A.copy(q_raw[:, r, :].rearrange("p (s f) -> p s f", s=S),
                       qk_ps[r % 2][:].rearrange("p (s f) -> p s f", s=S)[:, :, 0:F]).then_inc(q_ready, 1)

            def take_vr(c, r):
                act.wait_ge(vr_in_psum, c + 1)
                wait(act, kvT_in_psum, c - U + 1)
                wait(act, topidx_ready, c - U + 1)
                A.copy(vr[:, r], vr_ps[:, 0:S * (F + E)].rearrange("p (s f) -> p s f", s=S)).then_inc(vr_ready, 1)

            def norms(c, r):
                act.wait_ge(clamped_ready, c + 1)
                wait(act, rnorm_ready, c - U + 1)
                A.activation(norm[:, r, :], clamped[:, r, :], ACT.Sqrt).then_inc(norm_ready, 1)

            def qT_copy(c, r):
                act.wait_ge(qT_in_psum, c + 1)
                wait(act, o_in_psum, c - U + 2)
                A.copy(qnT[:, r, :], turn_ps[:, 0:S * P]).then_inc(qT_ready, 1)

            def mat_copy(c, r):
                act.wait_ge(mat_in_psum, c + 1)
                wait(act, o_in_psum, c - U + 2)
                A.copy(mat[:, r, :], mat_ps[:, 0:F]).then_inc(mat_ready, 1)

            def row_features(c, r):
                after_round(act, scattered, c, r, 16 * S)
                act.wait_ge(xn_ready, S * c + S)
                A.copy(rows[:, r, :, 0:F], xn[:, r, :].rearrange("p (s f) -> p s f", s=S)).then_inc(rown_ready, 1)

            def step1(i, r):
                stage(U, i, r, 7, NB, take_qk)
                stage(U, i, r, 9, NB, qT_copy)
                stage(U, i, r, 6, NB, take_vr)
                stage(U, i, r, 4, NB, normalise(0))
                stage(U, i, r, 0, NB, std_of)
                stage(U, i, r, 7, NB, norms)
                stage(U, i, r, 5, NB, xT_copy)
                stage(U, i, r, 7, NB, row_features)
                stage(U, i, r, 9, NB, mat_copy)
                if isinstance(i, int) and i == NB + 8:
                    act.wait_ge(ends_ready, 1)
                    write_pads(act, range(E // 2, E))
                stage(U, i, r, 4, NB, normalise(1))

            steps(act, U, HEAD1, NB, END1, step1)

            A.activation(m_work[:, 1, 0:1], eps[:], ACT.Gelu)

            def tanh(j, r):
                act.wait_ge(g_loaded[r], (j - r) // U2 * 16 + 16)
                wait(act, weight_ready, j - U2 + 1)
                A.activation(tanh_gap[:, r, :], grows[:, r, GAP:GAP + 1], ACT.Tanh, scale=0.5).then_inc(tanh_ready, 1)

            def gelu(j, r):
                act.wait_ge(h_in_psum, j + 1)
                wait(act, y_in_psum, j - U2 + 1)
                A.activation(hT[:, r, :], h_ps[r % 2][:], ACT.Gelu).then_inc(hT_ready, 1)

            def step2(i, r):
                stage(U2, i, r, 0, FT, tanh)
                stage(U2, i, r, 2, FT, gelu)

            steps(act, U2, HEAD2, FT, END2, step2)

        @block.vector
        def _(dve):
            V = nc.vector
            links = [0]

            def link(ins):
                links[0] += 1
                ins.then_inc(dve_chain, 1)
                dve.wait_ge(dve_chain, links[0])

            def split_biases(n):
                if n == 0:
                    dve.wait_ge(bias_loaded, 16 * 4)
                    dve.wait_ge(consts_pool, 3)
                    link(V.memset(bias3[:, 3 * F:3 * F + E], 0.0))
                rest = rest3[:, n - 1, :] if n else bias3[:]
                if n == 2:
                    V.tensor_copy(bias_parts[:], rest).then_inc(bias_ready, 1)
                else:
                    link(V.tensor_copy(part3[:, n, :], rest))
                    link(V.scalar_tensor_tensor(out=rest3[:, n, :], in0=part3[:, n, :], scalar=below[:, n:n + 1],
                                                in1=rest, op0=ALU.mult, op1=ALU.add))

            def sigmoid_of_m():
                dve.wait_ge(exp_m, 1)
                link(V.tensor_scalar(m_work[:, 1, :], m_work[:, 0, :], 1.0, None, ALU.add))
                V.reciprocal(m_work[:, 2, :], m_work[:, 1, :]).then_inc(sigmoid_m, 1)

            def scale_matrix():
                link(V.tensor_scalar(rowi[:, 1:2], rowi[:, 0:1], 3, None, ALU.arith_shift_right))
                link(V.tensor_scalar(coli[:, 1, :], coli[:, 0, :], 3, None, ALU.arith_shift_right))
                link(V.tensor_copy(rowf[:], rowi[:, 1:2]))
                link(V.tensor_scalar(same_head[:], coli[:, 1, :], rowf[:, 0:1], None, ALU.is_equal))
                dve.wait_ge(exp_m, 2)
                V.tensor_tensor(heads(head_scale[:]), heads(same_head[:]),
                                m_work[:, 3, :].unsqueeze(2).broadcast_to([P, H, HD]), ALU.mult).then_inc(scale_ready, 1)

            def statistics(c, r):
                if isinstance(c, int):
                    dve.wait_ge(x_loaded[[c in load for load in X_LOADS].index(True)], 16)
                if isinstance(c, int) and c == HEAD1 - 1:
                    for n, load in enumerate(X_LOADS):
                        if load.stop > HEAD1:
                            dve.wait_ge(x_loaded[n], 16)
                wait(dve, meanvar_ready, c - U + 1)
                for s in range(S):
                    ins = V.bn_stats(stats[:, r, s, :], one(x_sb[:, bass.ds(c, 1), s * F:(s + 1) * F]))
                ins.then_inc(stats_ready, 1)

            def aggregate(c, r):
                fixed_first(dve, x_loaded[0], 16, c + 1, (c - r) // U)
                dve.wait_ge(stats_ready, c + 1)
                wait(dve, shift_ready, (c - r) // U)
                for s in range(S):
                    ins = V.bn_aggr(meanvar[:, r, s, :], stats[:, r, s, :])
                ins.then_inc(meanvar_ready, 1)

            def rstd_of(c, r):
                if r != U - 1:
                    return
                dve.wait_ge(std_ready, (c - r) // U + 1)
                V.reciprocal(rstd[:, bass.ds((c - r) * S, U * S)], std[:]).then_inc(rstd_ready, 1)

            def shift_of(c, r):
                if r != U - 1:
                    return
                dve.wait_ge(rstd_ready, (c - r) // U + 1)
                t = bass.ds((c - r) * S, U * S)
                V.scalar_tensor_tensor(out=shift[:, t], in0=meanvar[:].rearrange("p u s t -> p (u s) t")[:, :, 0],
                                       scalar=-1.0, in1=rstd[:, t], op0=ALU.mult, op1=ALU.mult
                                       ).then_inc(shift_ready, 1)

            def sum_squares(c, r):
                dve.wait_ge(squares_ready, c + 1)
                wait(dve, clamped_ready, c - U + 1)
                V.tensor_reduce(sumsq[:, r, :], heads(squares[:, r, :]), AX.X, ALU.add).then_inc(sumsq_ready, 1)

            def top(c, r):
                fixed_first(dve, consts_pool, 3, c + 1, c - U + 1)
                dve.wait_ge(vr_ready, c + 1)
                wait(dve, gap_ready, c - U + 1)
                for s in range(S):
                    ins = V.max(top8[:, r, s, :], vr[:, r, s, F:F + E])
                ins.then_inc(top_ready, 1)

            def top_index(c, r):
                fixed_first(dve, consts_pool, 3, c + 1, c - U + 1)
                dve.wait_ge(top_ready, c + 1)
                wait(dve, onehot_ready, c - U + 1)
                for s in range(S):
                    ins = V.max_index(topidx[:, r, s, :], top8[:, r, s, :], vr[:, r, s, F:F + E])
                ins.then_inc(topidx_ready, 1)

            def one_hot(c, r):
                dve.wait_ge(topidx_ready, c + 1)
                wait(dve, seen_ready, c - U + 1)
                V.tensor_tensor(onehot[:, r], expert_no[:].unsqueeze(1).broadcast_to([P, S, E]),
                                topidx[:, r, :, 0:1].broadcast_to([P, S, E]), ALU.is_equal).then_inc(onehot_ready, 1)

            def mask_prefix(c, r):
                dve.wait_ge(prefix_in_psum, c + 1)
                wait(dve, place_ready, c - U + 1)
                V.tensor_tensor(prefix1[:, r], place_ps[:, 0:S * E].rearrange("p (s e) -> p s e", s=S),
                                onehot[:, r], ALU.mult).then_inc(prefix1_ready, 1)
                wait(dve, seen_ready, c)
                V.tensor_tensor(seen[:], seen[:], onehot[:, r], ALU.add).then_inc(seen_ready, 1)

            def find_place(c, r):
                dve.wait_ge(prefix1_ready, c + 1)
                after_round(dve, scattered, c, r, 16 * S)
                V.tensor_reduce(place[:, r, :], prefix1[:, r], AX.X, ALU.add).then_inc(place_ready, 1)

            def clamp(c, r):
                dve.wait_ge(sumsq_ready, c + 1)
                wait(dve, norm_ready, c - U + 1)
                V.tensor_scalar(clamped[:, r, :], sumsq[:, r, :], 1e-24, None, ALU.max).then_inc(clamped_ready, 1)

            def reciprocal_norms(c, r):
                dve.wait_ge(norm_ready, c + 1)
                wait(dve, qn_ready, c - U + 1)
                wait(dve, kn_ready, c - U + 1)
                V.reciprocal(rnorm[:, r].rearrange("p s h -> p (s h)"), norm[:, r, :]).then_inc(rnorm_ready, 1)

            def scale_k(c, r):
                dve.wait_ge(rnorm_ready, c + 1)
                dve.wait_ge(q_ready, c + 1)
                wait(dve, kvT_in_psum, c - U + 1)
                V.tensor_tensor(kn[:, r, :].rearrange("p (s g d) -> p s g d", s=S, d=HD),
                                qk_ps[r % 2][:].rearrange("p (s g d) -> p s g d", s=S, d=HD)[:, :, H:2 * H, :],
                                rnorm[:, r, :, H:2 * H].unsqueeze(3).broadcast_to([P, S, H, HD]),
                                ALU.mult).then_inc(kn_ready, 1)

            def mask_kvT(c, r):
                dve.wait_ge(kvT_in_psum, c + 1)
                wait(dve, mat_in_psum, c - U + 2)
                V.tensor_tensor(kvT[:, r, :], kvT_ps[:, 0:F], head_scale[:], ALU.mult).then_inc(kvT_ready, 1)

            def add_attention(c, r):
                dve.wait_ge(o_in_psum, c + 1)
                dve.wait_ge(info_ready, c + 1)
                V.tensor_tensor(rows[:, r, :, F:2 * F], o_ps[:, 0:S * F].rearrange("p (s f) -> p s f", s=S),
                                one(x_sb[:, bass.ds(c, 1), :]).rearrange("p (s f) -> p s f", s=S), ALU.add
                                ).then_inc(sum_ready, 1)

            def list_ends():
                dve.wait_ge(ends_in_psum, 1)
                V.tensor_copy(ends_i[:], place_ps[0:1, 0:E]).then_inc(ends_ready, 1)

            def tile_table():
                dve.wait_ge(ends_in_psum, 1)
                link(V.tensor_scalar(up_i[:, 0, :], place_ps[:, 0:E], float(P - 1), None, ALU.add))
                link(V.tensor_scalar(up_i[:, 1, :], up_i[:, 0, :], P.bit_length() - 1, None, ALU.arith_shift_right))
                link(V.tensor_tensor(tiles[:, 0, :], up_i[:, 1, :], first_tile[:], ALU.subtract))
                V.tensor_scalar(tiles[:, 2, :], tiles[:, 0, :], -float(P), float(REGION), ALU.mult, ALU.add)
                link(V.tensor_tensor_scan(tiles[:, 1, :], ones8[:], tiles[:, 0, :], 0.0, ALU.mult, ALU.add))
                link(V.tensor_scalar(reached[:, 0, :], tiles[:, 1, :], tile_no[:], None, ALU.is_le))
                V.tensor_reduce(entry[:, 0:1], reached[:, 0, :], AX.X, ALU.add)
                link(V.tensor_tensor(reached[:, 1, :], reached[:, 0, :], tiles[:, 2, :], ALU.mult))
                link(V.tensor_reduce(entry[:, 1:2], reached[:, 1, :], AX.X, ALU.add))
                link(V.scalar_tensor_tensor(out=entry[:, 2:3], in0=tile_no[:], scalar=float(P), in1=entry[:, 1:2],
                                            op0=ALU.mult, op1=ALU.add))
                V.tensor_scalar(entry[:, 3:4], entry[:, 0:1], float(E - 1), None, ALU.min)
                V.tensor_scalar(entry[:, 4:5], entry[:, 2:3], float(E * REGION), None, ALU.min
                                ).then_inc(entries_ready, 1)

            def table_copy():
                dve.wait_ge(table_in_psum, 1)
                V.tensor_copy(table[:], place_ps[0:1, 0:2 * P].rearrange("p (a b) -> p a b", a=2)
                              ).then_inc(table_ready, 1)

            def step1(i, r):
                if isinstance(i, int) and i == 1:
                    sigmoid_of_m()
                if isinstance(i, int) and i == U:
                    split_biases(1)
                    split_biases(2)
                if isinstance(i, int) and i == U + 1:
                    scale_matrix()
                stage(U, i, r, 0, NB, statistics)
                stage(U, i, r, 9, NB, mask_kvT)
                stage(U, i, r, 7, NB, sum_squares)
                stage(U, i, r, 10, NB, add_attention)
                stage(U, i, r, 0, NB, aggregate)
                if isinstance(i, int) and i == U - 1:
                    split_biases(0)
                stage(U, i, r, 7, NB, top)
                stage(U, i, r, 7, NB, clamp)
                stage(U, i, r, 8, NB, mask_prefix)
                stage(U, i, r, 7, NB, top_index)
                stage(U, i, r, 7, NB, one_hot)
                stage(U, i, r, 7, NB, reciprocal_norms)
                stage(U, i, r, 8, NB, find_place)
                stage(U, i, r, 0, NB, rstd_of)
                stage(U, i, r, 7, NB, scale_k)
                stage(U, i, r, 0, NB, shift_of)
                if isinstance(i, int) and i == NB + 7:
                    list_ends()
                if isinstance(i, int) and i == NB + 8:
                    tile_table()
                if isinstance(i, int) and i == NB + 9:
                    table_copy()

            steps(dve, U, HEAD1, NB, END1, step1)

            dve.wait_ge(ffn_loaded, 16 * 2 * E)

            def stage_w1(j, r):
                e = dve.value_load(table[0:1, 0, bass.ds(j, 1)], min_val=0, max_val=E - 1)
                wait(dve, h_in_psum, j - U2 + 1)
                V.tensor_copy(w1_now[:, r, :], one(w1_sb[:, bass.ds(e, 1), :])).then_inc(w1_staged, 1)

            def gT_copy(j, r):
                dve.wait_ge(gT_in_psum, j + 1)
                wait(dve, h_in_psum, j - U2 + 1)
                V.tensor_copy(gT[:, r, :], gT_ps[r % 2][:, 0:P]).then_inc(gT_ready, 1)

            def token_of(j, r):
                dve.wait_ge(g_loaded[r], (j - r) // U2 * 16 + 16)
                after_round(dve, stored, j, r, 16)
                V.tensor_copy(token[:, r, :], grows[:, r, TOK:TOK + 1]).then_inc(token_ready, 1)

            def weight_of(j, r):
                dve.wait_ge(tanh_ready, j + 1)
                wait(dve, orows_ready, j - U2 + 1)
                V.tensor_scalar(weight[:, r, :], tanh_gap[:, r, :], 0.5, 0.5, ALU.mult, ALU.add
                                ).then_inc(weight_ready, 1)

            def finish(j, r):
                dve.wait_ge(y_in_psum, j + 1)
                dve.wait_ge(weight_ready, j + 1)
                after_round(dve, stored, j, r, 16)
                V.scalar_tensor_tensor(out=orows[:, r, :], in0=y_ps[r % 2][:, 0:F], scalar=weight[:, r, :],
                                       in1=grows[:, r, F:2 * F], op0=ALU.mult, op1=ALU.add
                                       ).then_inc(orows_ready, 1)

            def step2(i, r):
                stage(U2, i, r, 0, FT, gT_copy)
                stage(U2, i, r, 0, FT, stage_w1)
                stage(U2, i, r, 2, FT, weight_of)
                stage(U2, i, r, 3, FT, finish)
                stage(U2, i, r, 0, FT, token_of)

            steps(dve, U2, HEAD2, FT, END2, step2)

        @block.tensor
        def _(pe):
            T = nc.tensor
            pe.wait_ge(consts_pool, 3)

            def warm_up(n):
                for _ in range(n):
                    T.matmul(place_ps[:, 0:P], ident[:], ident[:], start=True, stop=True)

            def transposes(c, r):
                pe.wait_ge(xn_ready, S * c + S)
                wait(pe, qT_ready, c - 3)
                for s in range(S):
                    ins = T.transpose(turn_ps[:, s * P:(s + 1) * P], xn[:, r, s * F:(s + 1) * F], ident[:])
                ins.then_inc(xT_in_psum, 1)

            def q_transposes(c, r):
                pe.wait_ge(qn_ready, c + 1)
                pe.wait_ge(xT_ready, c + 4 if not isinstance(c, int) else min(c + 4, NB))
                wait(pe, qT_ready, c)
                for s in range(S):
                    ins = T.transpose(turn_ps[:, s * P:(s + 1) * P], qn[:, r, s * F:(s + 1) * F], ident[:])
                ins.then_inc(qT_in_psum, 1)

            def bias_of(first, n):
                return bias_parts[:, first:first + n].unsqueeze(1).broadcast_to([3, S, n])

            def project_vr(c, r):
                if isinstance(c, int) and c == 0:
                    pe.wait_ge(bias_ready, 1)
                    pe.wait_ge(w_loaded, 16 * 5)
                pe.wait_ge(xT_ready, c + 1)
                wait(pe, vr_ready, c)
                T.matmul(vr_ps[:, 0:S * (F + E)], ones[0:3, :], bias_of(2 * F, F + E), start=True, stop=False)
                for s in range(S):
                    ins = T.matmul(vr_ps[:, s * (F + E):(s + 1) * (F + E)], xnT[:, r, s * P:(s + 1) * P], wvr[:],
                                   start=False, stop=(s == S - 1))
                ins.then_inc(vr_in_psum, 1)

            def project_qk(c, r):
                wait(pe, kn_ready, c - 1)
                T.matmul(qk_ps[r % 2][:], ones[0:3, :], bias_of(0, 2 * F), start=True, stop=False)
                for s in range(S):
                    ins = T.matmul(qk_ps[r % 2][:, s * 2 * F:(s + 1) * 2 * F], xnT[:, r, s * P:(s + 1) * P], wqk[:],
                                   start=False, stop=(s == S - 1))
                ins.then_inc(qk_in_psum, 1)

            def earlier_tokens(last):
                T.matmul(place_ps[:, 0:S * E], ones[0:1, :], region0[0:1], start=True, stop=False)
                for s in range(S):
                    ins = T.matmul(place_ps[:, 0:S * E], ones[:], seen[:, s:s + 1, :].broadcast_to([P, S, E]),
                                   start=False, stop=last and s == S - 1)
                return ins

            def prefixes(c, r):
                pe.wait_ge(onehot_ready, c + 1)
                wait(pe, seen_ready, c)
                wait(pe, prefix1_ready, c)
                earlier_tokens(False)
                T.matmul(place_ps[:, E:2 * E], ones[:], onehot[:, r, 0, :], start=False, stop=False)
                T.matmul(place_ps[:, 0:S * E], tri[:], onehot[:, r], start=False, stop=True
                         ).then_inc(prefix_in_psum, 1)

            def kv_product(c, r):
                pe.wait_ge(kn_ready, c + 1)
                pe.wait_ge(vr_ready, c + 1)
                wait(pe, kvT_ready, c)
                for s in range(S):
                    ins = T.matmul(kvT_ps[:, 0:F], vr[:, r, s, 0:F], kn[:, r, s * F:(s + 1) * F],
                                   start=(s == 0), stop=(s == S - 1))
                ins.then_inc(kvT_in_psum, 1)

            def with_wo(c, r):
                pe.wait_ge(kvT_ready, c + 1)
                wait(pe, mat_ready, c)
                T.matmul(mat_ps[:, 0:F], kvT[:, r, :], wo[:], start=True, stop=True).then_inc(mat_in_psum, 1)

            def attend(c, r):
                pe.wait_ge(qT_ready, c + 1)
                pe.wait_ge(mat_ready, c + 1)
                wait(pe, sum_ready, c)
                T.matmul(o_ps[:, 0:S * F], ones[0:3, :], bias_of(NBIAS - F, F), start=True, stop=False)
                for s in range(S):
                    ins = T.matmul(o_ps[:, s * F:(s + 1) * F], qnT[:, r, s * P:(s + 1) * P], mat[:, r, :],
                                   start=False, stop=(s == S - 1))
                ins.then_inc(o_in_psum, 1)

            def step1(i, r):
                stage(U, i, r, 6, NB, project_vr)
                stage(U, i, r, 8, NB, prefixes)
                stage(U, i, r, 10, NB, attend)
                stage(U, i, r, 6, NB, project_qk)
                stage(U, i, r, 5, NB, transposes)
                if isinstance(i, int) and i in WARM_UP:
                    warm_up(WARM_UP[i])
                stage(U, i, r, 8, NB, kv_product)
                stage(U, i, r, 9, NB, with_wo)
                stage(U, i, r, 8, NB, q_transposes)
                if isinstance(i, int) and i == NB + 7:
                    pe.wait_ge(seen_ready, NB)
                    pe.wait_ge(prefix1_ready, NB)
                    earlier_tokens(True).then_inc(ends_in_psum, 1)
                if isinstance(i, int) and i == NB + 9:
                    pe.wait_ge(entries_ready, 1)
                    for n in range(2):
                        ins = T.matmul(place_ps[0:1, n * P:(n + 1) * P], entry[:, 3 + n:4 + n], ident[:],
                                       start=True, stop=True)
                    ins.then_inc(table_in_psum, 1)

            steps(pe, U, HEAD1, NB, END1, step1)

            pe.wait_ge(table_ready, 1)
            warm_up(WARM_UP[FT])
            pe.wait_ge(ffn_loaded, 16 * 2 * E)
            pe.wait_ge(qT_ready, NB)
            pe.wait_ge(kvT_ready, NB)
            pe.wait_ge(mat_ready, NB)
            pe.wait_ge(sum_ready, NB)

            def g_transpose(j, r):
                pe.wait_ge(g_loaded[r], (j - r) // U2 * 16 + 16)
                wait(pe, gT_ready, j - 1)
                T.transpose(gT_ps[r % 2][:, 0:P], grows[:, r, 0:F], ident[:]).then_inc(gT_in_psum, 1)

            def up(j, r):
                pe.wait_ge(gT_ready, j + 1)
                pe.wait_ge(w1_staged, j + 1)
                wait(pe, hT_ready, j - 1)
                for n in range(HC):
                    ins = T.matmul(h_ps[r % 2][:, n * P:(n + 1) * P], w1_now[:, r, n * P:(n + 1) * P],
                                   gT[:, r, :], start=True, stop=True)
                ins.then_inc(h_in_psum, 1)

            def down(j, r):
                e = pe.value_load(table[0:1, 0, bass.ds(j, 1)], min_val=0, max_val=E - 1)
                pe.wait_ge(hT_ready, j + 1)
                wait(pe, orows_ready, j - 1)
                for n in range(HC):
                    ins = T.matmul(y_ps[r % 2][:, 0:F], hT[:, r, n * P:(n + 1) * P],
                                   one(w2_sb[:, bass.ds(e, 1), n * F:(n + 1) * F]),
                                   start=(n == 0), stop=(n == HC - 1))
                ins.then_inc(y_in_psum, 1)

            def step2(i, r):
                stage(U2, i, r, 0, FT, g_transpose)
                stage(U2, i, r, 2, FT, up)
                stage(U2, i, r, 3, FT, down)

            steps(pe, U2, HEAD2, FT, END2, step2)


_INS = ["L0_attn_x", "L0_attn_Wq", "L0_attn_bq", "L0_attn_Wk", "L0_attn_bk", "L0_attn_Wv", "L0_attn_bv",
        "L0_attn_Wo", "L0_attn_bo", "L0_attn_m", "L0_ffn_Wr", "L0_ffn_W1", "L0_ffn_W2"]
_OUTS = [((NB, NT, F), "float32")]


def kernel(**inputs):
    import numpy as _np
    import concourse.bacc as _bacc
    from concourse import mybir as _mybir
    from concourse.bass_utils import run_bass_kernel_spmd as _run

    nc = _bacc.Bacc("TRN2", target_bir_lowering=False, num_devices=1)
    arrays, args = {}, []
    for name in _INS:
        a = _np.ascontiguousarray(inputs[name])
        arrays[f"in_{name}_dram"] = a
        args.append(nc.dram_tensor(f"in_{name}_dram", a.shape, _mybir.dt.from_np(a.dtype), kind="ExternalInput").ap())
    for i, (shape, dtype) in enumerate(_OUTS):
        dt = _mybir.dt.from_np(_np.dtype(dtype))
        args.append(nc.dram_tensor(f"out_{i}_dram", shape, dt, kind="ExternalOutput").ap())
    block_kernel(nc, *args)
    r = _run(nc, [arrays], core_ids=[0])
    got = tuple(r.results[0][f"out_{i}_dram"] for i in range(len(_OUTS)))
    return got[0]
```
